# Optimizing a Trainium2 kernel written in Bass

```python
import numpy as np
import jax
import jax.numpy as jnp

def _softmax(x, axis=-1):
    return jax.nn.softmax(x, axis=axis)

def _gelu(x):
    return jax.nn.gelu(x, approximate=True)

def _silu(x):
    return jax.nn.silu(x)

def _sigmoid(x):
    return jax.nn.sigmoid(x)

def _layernorm(x, axis=-1, eps=1e-05):
    m = jnp.mean(x, axis=axis, keepdims=True)
    v = jnp.var(x, axis=axis, keepdims=True)
    return (x - m) / jnp.sqrt(v + eps)

def _scatter_add(tgt, idx, src, axis=0):
    return tgt.at[idx].add(src)

def _segment_sum(src, seg, n):
    return jax.ops.segment_sum(src, seg, n)
kernel_name = 'mk_decoder_preln_d1_seqx_r4_10c95d'

def setup_inputs(seed: int=0):
    np.random.seed(seed)
    _w = jnp.asarray

    def _rec_inputs():
        import jax
        import jax.numpy as jnp
        _rk = jax.random.key(seed)
        x = 0.0001212 + 1 * jax.random.normal(jax.random.fold_in(_rk, 1), (16, 128, 512), jnp.float32)
        _lenS = 128 - jax.random.randint(jax.random.fold_in(_rk, 7), (16,), 0, max(1, 128 // 4) + 1, jnp.int32)
        _lenS2 = 128 - jax.random.randint(jax.random.fold_in(_rk, 8), (16,), 0, max(1, 128 // 4) + 1, jnp.int32)
        _ctx_2048P = jax.random.normal(jax.random.fold_in(_rk, 11), (16, 16, 512), jnp.float32)
        _ctx_2048c = jax.random.dirichlet(jax.random.fold_in(_rk, 511), 0.3 * jnp.ones((16,), jnp.float32), (16, 128))
        _ctx_2048t = jnp.einsum('bsk,bkd->bsd', _ctx_2048c, _ctx_2048P)
        _ctx_2048t = _ctx_2048t * jax.lax.rsqrt(jnp.mean(jnp.square(_ctx_2048t)) + 1e-12) * 0.953939
        ctx_2048 = 0.000173663 + 1.0001 * (_ctx_2048t + 0.3 * jax.random.normal(jax.random.fold_in(_rk, 611), (16, 128, 512), jnp.float32))
        return (x, ctx_2048)
    x, ctx_2048 = _rec_inputs()

    def _L0_attn_setup():
        import jax, jax.numpy as jnp
        import numpy as np
        B, T, D_MODEL = (2, 512, 512)
        N_HEADS, D_HEAD = (16, 128)
        MAX_SEQ_LEN = 512
        LOGIT_SOFTCAP = 50.0
        EPS = 1e-06

        def precompute_rope(dim, max_seq_len, theta=10000.0):
            freqs = 1.0 / theta ** (np.arange(0, dim, 2, dtype=np.float32) / dim)
            t = np.arange(max_seq_len, dtype=np.float32)
            angles = np.outer(t, freqs)
            return (jnp.asarray(np.cos(angles)), jnp.asarray(np.sin(angles)))

        def rmsnorm(x, w):
            return x * jax.lax.rsqrt(jnp.mean(x * x, axis=-1, keepdims=True) + EPS) * w

        def apply_rope(x, cos, sin):
            n = x.shape[1]
            x1, x2 = (x[..., ::2], x[..., 1::2])
            c = cos[:n][None, :, None, :]
            s = sin[:n][None, :, None, :]
            out = jnp.stack([x1 * c - x2 * s, x1 * s + x2 * c], axis=-1)
            return out.reshape(x.shape)
        key = jax.random.key(seed)
        ks = jax.random.split(key, 6)
        x = jax.random.normal(ks[0], (B, T, D_MODEL), dtype=jnp.float32)
        wq = 0.02 * jax.random.normal(ks[1], (N_HEADS * D_HEAD, D_MODEL), dtype=jnp.float32)
        wk = 0.02 * jax.random.normal(ks[2], (N_HEADS * D_HEAD, D_MODEL), dtype=jnp.float32)
        wv = 0.02 * jax.random.normal(ks[3], (N_HEADS * D_HEAD, D_MODEL), dtype=jnp.float32)
        wo = 0.02 * jax.random.normal(ks[4], (D_MODEL, N_HEADS * D_HEAD), dtype=jnp.float32)
        q_norm_w = jnp.ones((D_HEAD,), dtype=jnp.float32)
        k_norm_w = jnp.ones((D_HEAD,), dtype=jnp.float32)
        rope_cos, rope_sin = precompute_rope(D_HEAD, MAX_SEQ_LEN)
        return {'x': x, 'wq': wq, 'wk': wk, 'wv': wv, 'wo': wo, 'q_norm_w': q_norm_w, 'k_norm_w': k_norm_w, 'rope_cos': rope_cos, 'rope_sin': rope_sin}
    _L0_attn_all = _L0_attn_setup()
    _L0_attn_in = {k: v for k, v in _L0_attn_all.items() if k in ('wq', 'wk', 'wv', 'wo', 'q_norm_w', 'k_norm_w', 'rope_cos', 'rope_sin')}
    del _L0_attn_all

    def _L0_xattn_setup():
        import jax, jax.numpy as jnp
        import numpy as np
        B_DIM, T_DIM, C_DIM = (16, 256, 512)

        def _wkv(w, u, k, v):
            Bn, Tn, Cn = k.shape
            NEG_INF = jnp.float32(-1e+38)

            def step(carry, kv_t):
                p, q, o = carry
                kt, vt = kv_t
                no = jnp.maximum(o, u + kt)
                A = jnp.exp(o - no)
                E = jnp.exp(u + kt - no)
                y = (A * p + E * vt) / (A * q + E)
                no2 = jnp.maximum(w + o, kt)
                A2 = jnp.exp(w + o - no2)
                E2 = jnp.exp(kt - no2)
                return ((A2 * p + E2 * vt, A2 * q + E2, no2), y)
            init = (jnp.zeros((Bn, Cn), k.dtype), jnp.zeros((Bn, Cn), k.dtype), jnp.full((Bn, Cn), NEG_INF, k.dtype))
            kT = jnp.moveaxis(k, 1, 0)
            vT = jnp.moveaxis(v, 1, 0)
            _, yT = jax.lax.scan(step, init, (kT, vT))
            return jnp.moveaxis(yT, 0, 1)
        key = jax.random.key(seed)
        k1, k2, k3, k4 = jax.random.split(key, 4)
        w = -jnp.exp(jax.random.normal(k1, (C_DIM,), jnp.float32))
        u = jax.random.normal(k2, (C_DIM,), jnp.float32)
        k = jax.random.normal(k3, (B_DIM, T_DIM, C_DIM), jnp.float32)
        v = jax.random.normal(k4, (B_DIM, T_DIM, C_DIM), jnp.float32)
        return {'B': B_DIM, 'T': T_DIM, 'C': C_DIM, 'w': w, 'u': u, 'k': k, 'v': v}
    _L0_xattn_all = _L0_xattn_setup()
    _L0_xattn_in = {k: v for k, v in _L0_xattn_all.items() if k in ('w', 'u')}
    del _L0_xattn_all

    def _L0_ffn_setup():
        import jax, jax.numpy as jnp
        import numpy as np
        H, I, E, TOP_K = (512, 352, 16, 6)
        IS = 704
        NORM_TOPK_PROB = False

        def _silu_and_mul(gate_up):
            d = gate_up.shape[-1] // 2
            g, u = (gate_up[..., :d], gate_up[..., d:])
            return jax.nn.silu(g) * u
        key = jax.random.key(seed)
        ks = jax.random.split(key, 6)
        s = 0.02
        return {'x': jax.random.normal(ks[0], (1, 512, H), jnp.float32), 'gate_w': jax.random.normal(ks[1], (E, H), jnp.float32) * s, 'w1': jax.random.normal(ks[2], (E, 2 * I, H), jnp.float32) * s, 'w2': jax.random.normal(ks[3], (E, H, I), jnp.float32) * s, 'shared_w1': jax.random.normal(ks[4], (2 * IS, H), jnp.float32) * s, 'shared_w2': jax.random.normal(ks[5], (H, IS), jnp.float32) * s}
    _L0_ffn_all = _L0_ffn_setup()
    _L0_ffn_in = {k: v for k, v in _L0_ffn_all.items() if k in ('gate_w', 'w1', 'w2', 'shared_w1', 'shared_w2')}
    del _L0_ffn_all
    return {'x': x, 'ctx_2048': ctx_2048, 'L0_attn_wq': _L0_attn_in['wq'], 'L0_attn_wk': _L0_attn_in['wk'], 'L0_attn_wv': _L0_attn_in['wv'], 'L0_attn_wo': _L0_attn_in['wo'], 'L0_attn_q_norm_w': _L0_attn_in['q_norm_w'], 'L0_attn_k_norm_w': _L0_attn_in['k_norm_w'], 'L0_attn_rope_cos': _L0_attn_in['rope_cos'], 'L0_attn_rope_sin': _L0_attn_in['rope_sin'], 'L0_xattn_w': _L0_xattn_in['w'], 'L0_xattn_u': _L0_xattn_in['u'], 'L0_ffn_gate_w': _L0_ffn_in['gate_w'], 'L0_ffn_w1': _L0_ffn_in['w1'], 'L0_ffn_w2': _L0_ffn_in['w2'], 'L0_ffn_shared_w1': _L0_ffn_in['shared_w1'], 'L0_ffn_shared_w2': _L0_ffn_in['shared_w2']}

def reference(x, ctx_2048, L0_attn_wq, L0_attn_wk, L0_attn_wv, L0_attn_wo, L0_attn_q_norm_w, L0_attn_k_norm_w, L0_attn_rope_cos, L0_attn_rope_sin, L0_xattn_w, L0_xattn_u, L0_ffn_gate_w, L0_ffn_w1, L0_ffn_w2, L0_ffn_shared_w1, L0_ffn_shared_w2):
    import jax
    import jax.numpy as jnp

    def _L0_attn_ref(x, wq, wk, wv, wo, q_norm_w, k_norm_w, rope_cos, rope_sin):
        import jax, jax.numpy as jnp
        import numpy as np
        B, T, D_MODEL = (2, 512, 512)
        N_HEADS, D_HEAD = (16, 128)
        MAX_SEQ_LEN = 512
        LOGIT_SOFTCAP = 50.0
        EPS = 1e-06

        def precompute_rope(dim, max_seq_len, theta=10000.0):
            freqs = 1.0 / theta ** (np.arange(0, dim, 2, dtype=np.float32) / dim)
            t = np.arange(max_seq_len, dtype=np.float32)
            angles = np.outer(t, freqs)
            return (jnp.asarray(np.cos(angles)), jnp.asarray(np.sin(angles)))

        def rmsnorm(x, w):
            return x * jax.lax.rsqrt(jnp.mean(x * x, axis=-1, keepdims=True) + EPS) * w

        def apply_rope(x, cos, sin):
            n = x.shape[1]
            x1, x2 = (x[..., ::2], x[..., 1::2])
            c = cos[:n][None, :, None, :]
            s = sin[:n][None, :, None, :]
            out = jnp.stack([x1 * c - x2 * s, x1 * s + x2 * c], axis=-1)
            return out.reshape(x.shape)
        Bx, Tx, _ = x.shape
        scale = D_HEAD ** (-0.5)
        q = (x @ wq.T).reshape(Bx, Tx, N_HEADS, D_HEAD).transpose(0, 2, 1, 3)
        k = (x @ wk.T).reshape(Bx, Tx, N_HEADS, D_HEAD).transpose(0, 2, 1, 3)
        v = (x @ wv.T).reshape(Bx, Tx, N_HEADS, D_HEAD).transpose(0, 2, 1, 3)
        q = rmsnorm(q, q_norm_w)
        k = rmsnorm(k, k_norm_w)
        q = apply_rope(q, rope_cos, rope_sin)
        k = apply_rope(k, rope_cos, rope_sin)
        scores = jnp.einsum('bhtd,bhsd->bhts', q, k) * scale
        scores = LOGIT_SOFTCAP * jnp.tanh(scores / LOGIT_SOFTCAP)
        mask = jnp.triu(jnp.ones((Tx, Tx), dtype=bool), k=1)
        scores = jnp.where(mask[None, None], -jnp.inf, scores)
        attn = jax.nn.softmax(scores, axis=-1)
        out = jnp.einsum('bhts,bhsd->bhtd', attn, v)
        out = out.transpose(0, 2, 1, 3).reshape(Bx, Tx, N_HEADS * D_HEAD)
        return out @ wo.T

    def _L0_xattn_ref(B, T, C, w, u, k, v):
        import jax, jax.numpy as jnp
        import numpy as np
        B_DIM, T_DIM, C_DIM = (16, 256, 512)

        def _wkv(w, u, k, v):
            Bn, Tn, Cn = k.shape
            NEG_INF = jnp.float32(-1e+38)

            def step(carry, kv_t):
                p, q, o = carry
                kt, vt = kv_t
                no = jnp.maximum(o, u + kt)
                A = jnp.exp(o - no)
                E = jnp.exp(u + kt - no)
                y = (A * p + E * vt) / (A * q + E)
                no2 = jnp.maximum(w + o, kt)
                A2 = jnp.exp(w + o - no2)
                E2 = jnp.exp(kt - no2)
                return ((A2 * p + E2 * vt, A2 * q + E2, no2), y)
            init = (jnp.zeros((Bn, Cn), k.dtype), jnp.zeros((Bn, Cn), k.dtype), jnp.full((Bn, Cn), NEG_INF, k.dtype))
            kT = jnp.moveaxis(k, 1, 0)
            vT = jnp.moveaxis(v, 1, 0)
            _, yT = jax.lax.scan(step, init, (kT, vT))
            return jnp.moveaxis(yT, 0, 1)
        return _wkv(w, u, k, v)

    def _L0_ffn_ref(x, gate_w, w1, w2, shared_w1, shared_w2):
        import jax, jax.numpy as jnp
        import numpy as np
        H, I, E, TOP_K = (512, 352, 16, 6)
        IS = 704
        NORM_TOPK_PROB = False

        def _silu_and_mul(gate_up):
            d = gate_up.shape[-1] // 2
            g, u = (gate_up[..., :d], gate_up[..., d:])
            return jax.nn.silu(g) * u
        B, S, Hd = x.shape
        xf = x.reshape(-1, Hd)
        T = xf.shape[0]
        shared_out = _silu_and_mul(xf @ shared_w1.T) @ shared_w2.T
        logits = xf @ gate_w.T
        probs = jax.nn.softmax(logits.astype(jnp.float32), axis=-1)
        routing_weights, selected = jax.lax.top_k(probs, TOP_K)
        if NORM_TOPK_PROB:
            routing_weights = routing_weights / routing_weights.sum(-1, keepdims=True)
        combine = jnp.zeros((T, E), jnp.float32).at[jnp.arange(T)[:, None], selected].add(routing_weights).astype(x.dtype)
        gate_up = jnp.einsum('th,eoh->teo', xf, w1)
        act = _silu_and_mul(gate_up)
        moe_out = jnp.einsum('te,tei,ehi->th', combine, act, w2)
        return (moe_out + shared_out).reshape(B, S, Hd)
    x = x + _L0_attn_ref(_layernorm(x, axis=-1), L0_attn_wq, L0_attn_wk, L0_attn_wv, L0_attn_wo, L0_attn_q_norm_w, L0_attn_k_norm_w, L0_attn_rope_cos, L0_attn_rope_sin)
    x = x + _L0_xattn_ref(16, 128, 512, L0_xattn_w, L0_xattn_u, _layernorm(x, axis=-1), ctx_2048)
    x = x + _L0_ffn_ref(_layernorm(x, axis=-1), L0_ffn_gate_w, L0_ffn_w1, L0_ffn_w2, L0_ffn_shared_w1, L0_ffn_shared_w2)
    return x

_drawn_inputs = setup_inputs


def setup_inputs(seed=0):
    import zlib

    import numpy as np

    out = dict(_drawn_inputs(seed))
    spreads = {'L0_attn_q_norm_w': (1.0, 0.6), 'L0_attn_k_norm_w': (1.0, 0.6)}
    factors = {'L0_ffn_gate_w': 8.0,
     'L0_ffn_w1': 7.157,
     'L0_ffn_w2': 7.185,
     'L0_ffn_shared_w1': 8.0,
     'L0_ffn_shared_w2': 8.0}
    for name, (base, spread) in spreads.items():
        noise = np.random.default_rng([zlib.crc32(name.encode()), seed]).standard_normal(out[name].shape)
        drawn = base * np.exp(spread * noise) if base else spread * noise
        out[name] = jnp.asarray(drawn.astype(out[name].dtype))
    for name, factor in factors.items():
        out[name] = (out[name] * factor).astype(out[name].dtype)
    return out
```

```python
from contextlib import ExitStack

import concourse.bass as bass
from concourse import mybir

F32 = mybir.dt.float32
F32R = mybir.dt.float32r
ACT = mybir.ActivationFunctionType
ALU = mybir.AluOpType
AX = mybir.AxisListType

P = 128
B, T, D = 16, 128, 512
NH, DH = 16, 128
E, TOPK, I = 16, 6, 352
NE = E + 2
KC = D // P
HG = 2
NG = NH // HG
IP = 384
IC = IP // P
NQ = B // 2
WCOLS = KC * 2 * I + IC * D
PIECE = WCOLS // B
QK_COLS, V_COLS = KC * 512, KC * 256
W2_AT = KC * 2 * I
NSTEP_B, NSTEP_F = NG * B, NE * B
LN_EPS, RMS_EPS = 1e-5, 1e-6
SCALE, CAP = DH ** -0.5, 50.0
NEG = -1e38
TERMS = ((0, 0), (0, 1), (1, 0))


def wait(eng, sem, count):
    if not isinstance(count, int) or count > 0:
        eng.wait_ge(sem, count)


def build(nc, x, ctxT, weights, qw, kw, cos2, sin2, wkv_w, wkv_u, gateT, out):
    xT_att = nc.dram_tensor("xT_att", (B, P, 2 * D), F32, kind="Internal").ap()
    xT_ffn = nc.dram_tensor("xT_ffn", (B, P, 2 * D), F32, kind="Internal").ap()

    with ExitStack() as ctx:
        def sb(name, shape, dt=F32):
            return ctx.enter_context(nc.sbuf_tensor(name, shape, dt))

        def sem(name):
            return ctx.enter_context(nc.semaphore(name))

        xres = sb("xres", [P, B, D])
        w_hl = [sb("w_hi", [P, 2, WCOLS], F32R), sb("w_lo", [P, 2, WCOLS], F32R)]
        raw = sb("raw", [P, 2, PIECE])
        xT = sb("xT", [P, 2, 2, D], F32R)
        ident = sb("ident", [P, P])
        comb = sb("comb", [P, NE, B])
        expo = sb("expo", [P, 4])
        st6 = sb("st6", [P, 2, 6])
        mv = sb("mv", [P, 2, 2])
        rstd = sb("rstd", [P, 2])
        xn = sb("xn", [P, 2, D])
        stage = sb("stage", [P, 2, 2, D], F32R)

        qkT = sb("qkT", [P, 2, 512], F32R)
        vE = sb("vE", [P, 2, 2, HG, 130], F32R)
        pT = sb("pT", [P, 2, HG, T], F32R)
        oT = sb("oT", [P, 2, HG, T], F32R)
        hT = sb("hT", [P, 2, IP], F32R)
        rope = sb("rope", [P, NH * DH])
        ssq = sb("ssq", [P, 4])
        rr = sb("rr", [P, 4])
        rk = sb("rk", [P, 2, HG])
        rden = sb("rden", [P, HG])
        hold = sb("hold", [P, 32])
        mask = sb("mask", [P, HG, T])
        kscale = sb("kscale", [P, HG])

        def seg(name):
            return sb(name, [P, KC * 2, T + 1])

        kS, oS, a2, e2, e2v, pS, qS, wrst = (seg(n) for n in ("kS", "oS", "a2", "e2", "e2v", "pS", "qS", "wrst"))
        dE, aA, vS = (sb(n, [P, KC * 2, T]) for n in ("dE", "aA", "vS"))
        wcol = sb("wcol", [P, KC])
        ucol = sb("ucol", [P, KC])
        gate = sb("gate", [P, KC, E])
        gate_hl = sb("gate_hl", [P, 2, KC, E], F32R)
        lg = sb("lg", [P, 2, E])
        pr = sb("pr", [P, 2, E])
        mx = sb("mx", [P, 2])
        sm = sb("sm", [P, 2])
        rsm = sb("rsm", [P, 2])
        m8 = sb("m8", [P, 2, 8])
        gt = sb("gt", [P, 2, E])
        eq = sb("eq", [P, 2, E])
        cnt = sb("cnt", [P, 2])
        rank = sb("rank", [P, 2, E])
        zero16 = sb("zero16", [P, E])

        def flat(t):
            return t[:, :, :].rearrange("p a b -> p (a b)")

        sq, rot = flat(a2)[:, 0:512], flat(e2)[:, 0:512]
        th, ex, on = flat(e2v)[:, 0:256], flat(pS)[:, 0:256], flat(qS)[:, 0:256]
        tg, a1, hid = flat(kS)[:, 0:I], flat(oS)[:, 0:I], flat(a2)[:, 0:IP]
        sin_in = [flat(kS)[:, 0:NH * DH // 2], flat(oS)[:, 0:NH * DH // 2]]
        qw_in, kw_in = flat(a2)[:, 0:DH], flat(e2)[:, 0:DH]

        bank = [ctx.enter_context(nc.psum_tensor(f"bank{i}", [P, 512], F32)) for i in range(8)]

        piece_in = [sem("piece_in0"), sem("piece_in1")]
        piece_hi, piece_lo = sem("piece_hi"), sem("piece_lo")
        stats_done, aggr_done, rstd_done, ln_done = sem("stats_done"), sem("aggr_done"), sem("rstd_done"), sem("ln_done")
        var_done = sem("var_done")

        ident_done = sem("ident_done")

        sites = []

        def wait_apart(dve, sem_, count):
            wait(dve, sem_, count)
            if not isinstance(count, int):
                sites.append(sem_)
                dve.tensor_copy(hold[:, len(sites):len(sites) + 1], hold[:, 0:1])

        def ln_vector(dve, k, b):
            for j in range(2):
                dve.bn_stats(st6[:, j, :], xres[:, b + j, :]).then_inc(stats_done, 1)
            for j in range(2):
                wait_apart(dve, stats_done, 2 * k + j + 1)
                dve.bn_aggr(mv[:, j, :], st6[:, j, :]).then_inc(aggr_done, 1)
            dve.wait_ge(aggr_done, 2 * k + 2)
            dve.tensor_scalar(rstd[:, :], mv[:, :, 1], LN_EPS, None, ALU.add).then_inc(var_done, 1)
            dve.wait_ge(rstd_done, k + 1)
            for j in range(2):
                dve.tensor_scalar(xn[:, j, :], xres[:, b + j, :], mv[:, j, 0:1], rstd[:, j:j + 1],
                                  ALU.subtract, ALU.mult).then_inc(ln_done, 1)

        def ln_pool(pool, k):
            pool.wait_ge(var_done, k + 1)
            pool.tensor_tensor(rstd[:, :], rstd[:, :], expo[:, 0:2], ALU.pow).then_inc(rstd_done, 1)

        def transposes(pe, out, src, done):
            for c in range(KC):
                last = pe.transpose(out[:, c * P:(c + 1) * P], src(c), ident[:, :])
            last.then_inc(done, 1)

        def piece_act(act, even, par, gpar, at):
            act.wait_ge(piece_in[par], 8 * even + 16)
            act.activation(w_hl[0][:, gpar, at], raw[:, par, :], ACT.Copy).then_inc(piece_hi, 1)

        def piece_pool(pool, number, par, gpar, at):
            pool.wait_ge(piece_hi, number + 1)
            pool.tensor_tensor(w_hl[1][:, gpar, at], raw[:, par, :], w_hl[0][:, gpar, at].bitcast(F32),
                               ALU.subtract).then_inc(piece_lo, 1)

        def looped(eng, body, n):
            body(0)
            with eng.Fori(1, n) as q:
                body(q)

        ld_x, ld_c, ld_t, consts = sem("ld_x"), sem("ld_c"), sem("ld_t"), sem("consts")
        trA, hiA, loA, stA, tabs = sem("trA"), sem("hiA"), sem("loA"), sem("stA"), sem("tabs")
        with nc.Block() as block:
            @block.sync
            def _(sp):
                half = NH * DH // 2
                for dst, src in ((rope[:, :], cos2), (sin_in[0], sin2[0:half]), (sin_in[1], sin2[half:]),
                                 (qw_in, qw), (kw_in, kw)):
                    sp.dma_start(dst, src.partition_broadcast(P)).then_inc(ld_t, 16)
                sp.dma_start(xres[:, :, :], x.rearrange("b t d -> t b d")).then_inc(ld_x, 16)
                for par in range(2):
                    sp.dma_start(raw[:, par, :], weights[par]).then_inc(piece_in[par], 16)
                for dst, src in ((wcol[:, :], wkv_w), (ucol[:, :], wkv_u), (flat(gate), gateT)):
                    sp.dma_start(dst, src).then_inc(ld_c, 16)

                def store(q):
                    for j in range(2):
                        sp.wait_ge(hiA, 2 * q + j + 1)
                        sp.wait_ge(loA, 2 * q + j + 1)
                        sp.dma_start(xT_att[2 * q + j],
                                     stage[:, j, :, :].rearrange("p h n -> p (h n)").bitcast(F32)).then_inc(stA, 16)

                with sp.Fori(0, NQ - 1) as q:
                    store(q)
                    for par in range(2):
                        sp.wait_ge(piece_lo, 2 * q + par + 1)
                        sp.dma_start(raw[:, par, :], weights[2 * q + 2 + par]).then_inc(piece_in[par], 16)
                store(NQ - 1)
                sp.wait_ge(stA, 16 * B)

            @block.scalar
            def _(act):
                def body(q):
                    for j in range(2):
                        act.wait_ge(trA, 2 * q + j + 1)
                        if j == 0:
                            wait(act, stA, 32 * q)
                        act.activation(stage[:, j, 0, :], bank[j][:, :], ACT.Copy).then_inc(hiA, 1)
                    for par in range(2):
                        piece_act(act, 2 * q, par, 0, bass.ds((2 * q + par) * PIECE, PIECE))
                looped(act, body, NQ)

            @block.gpsimd
            def _(pool):
                pool.memset(expo[:, :], -0.5).then_inc(consts, 1)
                pool.memset(ident[:, :], 0.0).then_inc(consts, 1)
                pool.wait_ge(consts, 2)
                pool.affine_select(out=ident[:, :], in_=ident[:, :], compare_op=ALU.not_equal, fill=1.0, base=0,
                                   pattern=[[-1, P]], channel_multiplier=1).then_inc(ident_done, 1)
                pool.memset(mask[:, :, :], 1.0).then_inc(consts, 1)
                pool.memset(kscale[:, :], SCALE / CAP).then_inc(consts, 1)
                pool.memset(hold[:, :], 0.0).then_inc(consts, 1)
                pool.wait_ge(consts, 5)
                pool.affine_select(out=mask[:, :, :], in_=mask[:, :, :], compare_op=ALU.is_ge, fill=0.0, base=0,
                                   pattern=[[0, HG], [1, T]], channel_multiplier=-1).then_inc(consts, 1)
                pool.memset(comb[:, E:NE, :], 0.5).then_inc(consts, 1)
                for par in range(2):
                    pool.memset(vE[:, par, 0, :, 128:129].bitcast(F32), 1.0).then_inc(consts, 1)
                    pool.memset(vE[:, par, 0, :, 129:130].bitcast(F32), 0.0).then_inc(consts, 1)
                    pool.memset(vE[:, par, 1, :, 128:130].bitcast(F32), 0.0).then_inc(consts, 1)

                def body(q):
                    ln_pool(pool, q)
                    for par in range(2):
                        piece_pool(pool, 2 * q + par, par, 0, bass.ds((2 * q + par) * PIECE, PIECE))
                looped(pool, body, NQ)

            @block.vector
            def _(dve):
                half = NH * DH // 2
                dve.wait_ge(ld_t, 80)
                dve.tensor_tensor(rope[:, :], rope[:, :], rope[:, :], ALU.mult).then_inc(tabs, 1)
                for i in range(2):
                    dve.tensor_tensor(sin_in[i], sin_in[i], sin_in[i], ALU.mult).then_inc(tabs, 1)
                dve.tensor_tensor(qw_in, qw_in, kw_in, ALU.mult).then_inc(tabs, 1)
                dve.wait_ge(tabs, 4)
                for i in range(2):
                    part = rope[:, i * half:(i + 1) * half]
                    dve.tensor_tensor(part, part, sin_in[i], ALU.add).then_inc(tabs, 1)
                dve.wait_ge(tabs, 6)
                all_heads = rope[:, :].rearrange("p (h d) -> p h d", h=NH)
                dve.tensor_tensor(all_heads, all_heads, qw_in.unsqueeze(1).to_broadcast([P, NH, DH]),
                                  ALU.mult).then_inc(tabs, 1)
                dve.wait_ge(ld_x, 16)
                dve.wait_ge(consts, 5)

                def body(q):
                    if isinstance(q, int):
                        ln_vector(dve, 0, 0)
                    else:
                        wait_apart(dve, trA, 2 * q)
                        ln_vector(dve, q, 2 * q)
                    for j in range(2):
                        dve.wait_ge(hiA, 2 * q + j + 1)
                        dve.tensor_tensor(stage[:, j, 1, :], bank[j][:, :], stage[:, j, 0, :].bitcast(F32),
                                          ALU.subtract).then_inc(loA, 1)
                looped(dve, body, NQ)
            @block.tensor
            def _(pe):
                pe.wait_ge(ident_done, 1)

                def body(q):
                    for j in range(2):
                        pe.wait_ge(ln_done, 2 * q + j + 1)
                        wait(pe, hiA, 2 * q + j - 1)
                        wait(pe, loA, 2 * q + j - 1)
                        transposes(pe, bank[j], lambda c: xn[:, j, c * P:(c + 1) * P], trA)
                body(0)
                with pe.Fori(1, NQ) as q:
                    body(q)

        xT_in = [sem("xT_in0"), sem("xT_in1")]
        (qk_done, s_done, ot_done, v_done, wo_done, pv_done, t_done, sq_done, th_done, ex_done, oT_hi, p_hi,
         v_hi, qkT_hi, k_out, ss_done, oT_lo, p_lo, v_lo, acc_done, rden_done, on_done, qkT_lo,
         mask_done, ms_done, pw_done, rms_done, rot_done) = (sem(n) for n in (
             "qk_done", "s_done", "ot_done", "v_done", "wo_done", "pv_done", "t_done", "sq_done", "th_done",
             "ex_done", "oT_hi", "p_hi", "v_hi", "qkT_hi", "k_out", "ss_done", "oT_lo", "p_lo", "v_lo",
             "acc_done", "rden_done", "on_done", "qkT_lo", "mask_done", "ms_done", "pw_done",
             "rms_done", "rot_done"))
        S_, OT_, V_, Y_, O_, QT_ = bank[2:8]
        heads = lambda ap: ap.rearrange("p (h n) -> p h n", h=HG)

        def attention(eng, step):
            for i in range(4):
                step(i, i % 2, i, 0, 0, 0, True, i > 0, i > 1, i > 2)

            def group(base, gp, last):
                with eng.Fori(4, B - 1, 2) as b:
                    s = eng.snap(base + b)
                    step(s, 0, b, base, gp, gp, True, True, True, True)
                    step(s + 1, 1, b + 1, base, gp, gp, True, True, True, True)
                for i in range(3 if last else 4):
                    step(base + B + i, i % 2, i, base + B, 1 - gp, gp if i < 3 else 1 - gp,
                         not last, not last or i < 1, not last or i < 2, True)

            with eng.Fori(0, NSTEP_B - 4 * B + 1, 2 * B) as base:
                group(base, 0, False)
                group(base + B, 1, False)
            group(NSTEP_B - 2 * B, 0, False)
            group(NSTEP_B - B, 1, True)

        with nc.Block() as block:
            @block.sync
            def _(sp):
                def step(s, par, b, first, fw, bw, front, mid, back, tail):
                    if not front:
                        return
                    wait(sp, v_done, s - 1)
                    sp.dma_start(xT[:, par, :, :].rearrange("p h n -> p (h n)").bitcast(F32),
                                 xT_att[b]).then_inc(xT_in[par], 16)
                    wait(sp, piece_lo, B + s - 1)
                    sp.dma_start(raw[:, par, :], weights[s + B]).then_inc(piece_in[par], 16)
                attention(sp, step)

            @block.tensor
            def _(pe):
                def step(s, par, b, first, fw, bw, front, mid, back, tail):
                    if front:
                        if isinstance(b, int) and b == 0:
                            pe.wait_ge(piece_hi, s + B)
                            pe.wait_ge(piece_lo, s + B)
                        pe.wait_ge(xT_in[par], 8 * (s - par) + 16)
                        n = 0
                        for c in range(KC):
                            for a, w in TERMS:
                                last = pe.matmul(bank[par][:, :], xT[:, par, a, c * P:(c + 1) * P],
                                                 w_hl[w][:, fw, c * 512:(c + 1) * 512],
                                                 start=n == 0, stop=n == 11)
                                n += 1
                        last.then_inc(qk_done, 1)
                    if mid:
                        pe.wait_ge(k_out, s)
                        pe.wait_ge(rot_done, 2 * s)
                        transposes(pe, QT_, lambda c: rot[:, c * P:(c + 1) * P], t_done)
                    if tail:
                        pe.wait_ge(oT_hi, s - 2)
                        pe.wait_ge(oT_lo, s - 2)
                        if not mid:
                            pe.wait_ge(acc_done, s - 3)
                        n = 0
                        for h in range(HG):
                            for a, w in TERMS:
                                at = QK_COLS + V_COLS + h * D
                                last = pe.matmul(Y_[:, :], oT[:, a, h, :], w_hl[w][:, bw, at:at + D],
                                                 start=n == 0, stop=n == 5)
                                n += 1
                        last.then_inc(wo_done, 1)
                    if back:
                        pe.wait_ge(p_hi, s - 1)
                        pe.wait_ge(p_lo, s - 1)
                        pe.wait_ge(v_hi, s - 1)
                        pe.wait_ge(v_lo, s - 1)
                        for h in range(HG):
                            for n, (a, w) in enumerate(TERMS):
                                last = pe.matmul(O_[:, h * 130:(h + 1) * 130], pT[:, a, h, :],
                                                 vE[:, par, w, h, :], start=n == 0, stop=n == 2)
                        last.then_inc(pv_done, 1)
                    if front:
                        wait(pe, v_hi, s)
                        wait(pe, v_lo, s)
                        n = 0
                        for c in range(KC):
                            for a, w in TERMS:
                                at = QK_COLS + c * 256
                                last = pe.matmul(V_[:, 0:256], xT[:, par, a, c * P:(c + 1) * P],
                                                 w_hl[w][:, fw, at:at + 256], start=n == 0, stop=n == 11)
                                n += 1
                        last.then_inc(v_done, 1)
                    if back:
                        pe.wait_ge(on_done, s - 1)
                        for h in range(HG):
                            last = pe.transpose(OT_[:, h * T:(h + 1) * T], on[:, h * DH:(h + 1) * DH], ident[:, :])
                        last.then_inc(ot_done, 1)
                    if mid:
                        pe.wait_ge(qkT_hi, s)
                        pe.wait_ge(qkT_lo, s)
                        wait(pe, th_done, 2 * s - 2)
                        for h in range(HG):
                            for n, (a, w) in enumerate(TERMS):
                                last = pe.matmul(S_[:, h * T:(h + 1) * T], qkT[:, a, (HG + h) * T:(HG + h + 1) * T],
                                                 qkT[:, w, h * T:(h + 1) * T], start=n == 0, stop=n == 2)
                        last.then_inc(s_done, 1)
                attention(pe, step)

            @block.scalar
            def _(act):
                def step(s, par, b, first, fw, bw, front, mid, back, tail):
                    if front:
                        act.wait_ge(qk_done, s + 1)
                        wait(act, ss_done, s)
                        act.activation(sq, bank[par][:, :], ACT.Square).then_inc(sq_done, 1)
                    if mid:
                        act.wait_ge(t_done, s)
                        act.activation(qkT[:, 0, :], QT_[:, :], ACT.Copy).then_inc(qkT_hi, 1)
                    if front:
                        act.activation(rot[:, 256:512], bank[par][:, 256:512], ACT.Copy).then_inc(k_out, 1)
                        piece_act(act, s + B - par, par, 1 - fw, bass.ds(b * PIECE, PIECE))
                        act.wait_ge(v_done, s + 1)
                        act.activation(vE[:, par, 0, :, 0:DH], heads(V_[:, 0:256]), ACT.Copy).then_inc(v_hi, 1)
                    if back:
                        act.wait_ge(ot_done, s - 1)
                        act.activation(oT[:, 0, :, :], heads(OT_[:, 0:256]), ACT.Copy).then_inc(oT_hi, 1)
                    if mid:
                        act.wait_ge(s_done, s)
                        act.wait_ge(rms_done, s)
                        for h in range(HG):
                            act.activation(th[:, h * T:(h + 1) * T], S_[:, h * T:(h + 1) * T], ACT.Tanh,
                                           scale=rk[:, 1 - par, h:h + 1]).then_inc(th_done, 1)
                        act.wait_ge(th_done, 2 * s)
                        wait(act, p_lo, s - 1)
                        act.activation(ex, th, ACT.Exp, scale=CAP).then_inc(ex_done, 1)
                        act.wait_ge(mask_done, s)
                        act.activation(pT[:, 0, :, :], heads(ex), ACT.Copy).then_inc(p_hi, 1)
                attention(act, step)

            @block.vector
            def _(dve):
                def step(s, par, b, first, fw, bw, front, mid, back, tail):
                    if front:
                        dve.wait_ge(sq_done, s + 1)
                        dve.reduce_sum(ssq[:, :], sq.rearrange("p (g n) -> p g n", g=4), AX.X).then_inc(ss_done, 1)
                    if mid:
                        dve.wait_ge(qkT_hi, s)
                        dve.tensor_tensor(qkT[:, 1, :], QT_[:, :], qkT[:, 0, :].bitcast(F32),
                                          ALU.subtract).then_inc(qkT_lo, 1)
                    if front:
                        wait(dve, rms_done, s)
                        dve.wait_ge(ss_done, s + 1)
                        dve.tensor_scalar(rr[:, :], ssq[:, :], 1.0 / DH, RMS_EPS, ALU.mult, ALU.add)\
                            .then_inc(ms_done, 1)
                    if tail:
                        dve.wait_ge(wo_done, s - 2)
                        bb = b - 3 if not isinstance(b, int) else (b - 3) % B
                        dve.tensor_tensor(xres[:, bb, :], xres[:, bb, :], Y_[:, :], ALU.add).then_inc(acc_done, 1)
                    if back:
                        dve.wait_ge(pv_done, s - 1)
                        av = O_[:, 0:HG * 130].rearrange("p (h n) -> p h n", h=HG)
                        dve.reciprocal(rden[:, :], av[:, :, DH]).then_inc(rden_done, 1)
                        dve.wait_ge(rden_done, s - 1)
                        dve.tensor_tensor(heads(on), av[:, :, 0:DH],
                                          rden[:, :].unsqueeze(2).to_broadcast([P, HG, DH]),
                                          ALU.mult).then_inc(on_done, 1)
                    if front:
                        dve.wait_ge(pw_done, s + 1)
                        dve.wait_ge(k_out, s + 1)
                        for h in range(HG):
                            at = first * (HG * DH // B) + h * DH
                            dve.scalar_tensor_tensor(out=rot[:, h * DH:(h + 1) * DH],
                                                     in0=bank[par][:, h * DH:(h + 1) * DH], scalar=rr[:, h:h + 1],
                                                     in1=rope[:, bass.ds(at, DH)], op0=ALU.mult,
                                                     op1=ALU.mult).then_inc(rot_done, 1)
                        dve.wait_ge(v_hi, s + 1)
                        dve.tensor_tensor(vE[:, par, 1, :, 0:DH], heads(V_[:, 0:256]),
                                          vE[:, par, 0, :, 0:DH].bitcast(F32), ALU.subtract).then_inc(v_lo, 1)
                    if back:
                        dve.wait_ge(oT_hi, s - 1)
                        dve.tensor_tensor(oT[:, 1, :, :], heads(OT_[:, 0:256]), oT[:, 0, :, :].bitcast(F32),
                                          ALU.subtract).then_inc(oT_lo, 1)
                    if mid:
                        dve.wait_ge(p_hi, s)
                        dve.tensor_tensor(pT[:, 1, :, :], heads(ex), pT[:, 0, :, :].bitcast(F32),
                                          ALU.subtract).then_inc(p_lo, 1)
                attention(dve, step)

            @block.gpsimd
            def _(pool):
                def step(s, par, b, first, fw, bw, front, mid, back, tail):
                    if front:
                        pool.wait_ge(ms_done, s + 1)
                        pool.tensor_tensor(rr[:, :], rr[:, :], expo[:, :], ALU.pow).then_inc(pw_done, 1)
                        wait(pool, th_done, 2 * s - 2)
                        pool.wait_ge(pw_done, s + 1)
                        pool.tensor_tensor(rk[:, par, :], rr[:, HG:4], kscale[:, :], ALU.mult).then_inc(rms_done, 1)
                        piece_pool(pool, s + B, par, 1 - fw, bass.ds(b * PIECE, PIECE))
                    if mid:
                        pool.wait_ge(ex_done, s)
                        pool.tensor_tensor(heads(ex), heads(ex), mask[:, :, :], ALU.mult).then_inc(mask_done, 1)
                attention(pool, step)

        (consW, trK, kT_in, o_scan, d2_done, e2a_done, d_done, emin, amin, a2_done, e2_done, aA_done, dE_done,
         v_in, e2v_done, ev_done, pscan, qscan, pm_done, qm_done, num_done, den_done, rec_done, y_done, trY,
         res_done, trX, hiW, loW, stW, gate_w, lg_done, lg_in, mx_done, lgs_done, ex16, sm_done, rs_done,
         pr_done, m8_done, gt_done, cnt_done, eq_done, rank_done, ok_done, sel_done, selg, comb_done) = (
             sem(n) for n in (
                 "consW", "trK", "kT_in", "o_scan", "d2_done", "e2a_done", "d_done", "emin", "amin", "a2_done",
                 "e2_done", "aA_done", "dE_done", "v_in", "e2v_done", "ev_done", "pscan", "qscan", "pm_done",
                 "qm_done", "num_done", "den_done", "rec_done", "y_done", "trY", "res_done", "trX", "hiW",
                 "loW", "stW", "gate_w", "lg_done", "lg_in", "mx_done", "lgs_done", "ex16", "sm_done",
                 "rs_done", "pr_done", "m8_done", "gt_done", "cnt_done", "eq_done", "rank_done", "ok_done",
                 "sel_done", "selg", "comb_done"))
        cj = lambda t, j: t[:, :, :].rearrange("p (c j) t -> p j c t", j=2)[:, j, :, :]
        with nc.Block() as block:
            @block.sync
            def _(sp):
                def body(q):
                    wait(sp, trY, 2 * q)
                    sp.dma_start(vS[:, :, :].rearrange("p a t -> p (a t)"), ctxT[q]).then_inc(v_in, 16)
                    for j in range(2):
                        sp.wait_ge(hiW, 2 * q + j + 1)
                        sp.wait_ge(loW, 2 * q + j + 1)
                        sp.dma_start(xT_ffn[2 * q + j],
                                     stage[:, j, :, :].rearrange("p h n -> p (h n)").bitcast(F32)).then_inc(stW, 16)
                looped(sp, body, NQ)
                sp.wait_ge(stW, 16 * B)

            @block.tensor
            def _(pe):
                def body(q):
                    for j in range(2):
                        pe.wait_ge(ln_done, B + 4 * q + j + 1)
                        wait(pe, kT_in, 2 * q)
                        transposes(pe, bank[j], lambda c: xn[:, j, c * P:(c + 1) * P], trK)
                    pe.wait_ge(y_done, q + 1)
                    wait(pe, res_done, 2 * q)
                    for j in range(2):
                        transposes(pe, bank[2 + j], lambda c: vS[:, 2 * c + j, :], trY)
                    for j in range(2):
                        pe.wait_ge(ln_done, B + 4 * q + 2 + j + 1)
                        wait(pe, loW, 2 * q)
                        transposes(pe, bank[4 + j], lambda c: xn[:, j, c * P:(c + 1) * P], trX)
                    wait(pe, lg_in, q)
                    if isinstance(q, int):
                        pe.wait_ge(gate_w, 2)
                    for j in range(2):
                        pe.wait_ge(hiW, 2 * q + j + 1)
                        pe.wait_ge(loW, 2 * q + j + 1)
                        n = 0
                        for c in range(KC):
                            for a, w in TERMS:
                                last = pe.matmul(bank[6][:, j * E:(j + 1) * E], stage[:, j, a, c * P:(c + 1) * P],
                                                 gate_hl[:, w, c, :], start=n == 0, stop=n == 11)
                                n += 1
                        last.then_inc(lg_done, 1)
                looped(pe, body, NQ)

            @block.scalar
            def _(act):
                act.activation(gate_hl[:, 0, :, :], gate[:, :, :], ACT.Copy).then_inc(gate_w, 1)

                def body(q):
                    wait(act, d_done, 4 * q)
                    wait(act, e2a_done, q)
                    for j in range(2):
                        act.wait_ge(trK, 2 * q + j + 1)
                        act.activation(cj(kS, j)[:, :, 1:T + 1],
                                       bank[j][:, :].rearrange("p (c t) -> p c t", c=KC), ACT.Copy).then_inc(kT_in, 1)
                    act.wait_ge(d2_done, 4 * q + 4)
                    act.activation(a2[:, :, 1:T + 1], a2[:, :, 1:T + 1], ACT.Exp).then_inc(a2_done, 1)
                    act.wait_ge(e2a_done, q + 1)
                    act.activation(e2[:, :, 1:T + 1], e2[:, :, 1:T + 1], ACT.Exp).then_inc(e2_done, 1)
                    act.wait_ge(amin, q + 1)
                    act.activation(aA[:, :, :], aA[:, :, :], ACT.Exp).then_inc(aA_done, 1)
                    act.wait_ge(emin, q + 1)
                    act.activation(dE[:, :, :], dE[:, :, :], ACT.Exp).then_inc(dE_done, 1)
                    for j in range(2):
                        act.wait_ge(trX, 2 * q + j + 1)
                        if j == 0:
                            wait(act, stW, 32 * q)
                            wait(act, lg_done, 2 * q)
                        act.activation(stage[:, j, 0, :], bank[4 + j][:, :], ACT.Copy).then_inc(hiW, 1)
                    act.wait_ge(lg_done, 2 * q + 2)
                    act.activation(lg[:, :, :], bank[6][:, 0:2 * E].rearrange("p (j e) -> p j e", j=2),
                                   ACT.Copy).then_inc(lg_in, 1)
                    act.wait_ge(lgs_done, q + 1)
                    act.activation(pr[:, :, :], lg[:, :, :], ACT.Exp).then_inc(ex16, 1)
                looped(act, body, NQ)

            @block.gpsimd
            def _(pool):
                def body(q):
                    ln_pool(pool, NQ + 2 * q)
                    pool.wait_ge(o_scan, q + 1)
                    wait(pool, qscan, q)
                    pool.tensor_tensor(e2[:, :, 1:T + 1], kS[:, :, 1:T + 1], oS[:, :, 1:T + 1],
                                       ALU.subtract).then_inc(e2a_done, 1)
                    pool.wait_ge(e2_done, q + 1)
                    pool.wait_ge(v_in, 16 * q + 16)
                    if isinstance(q, int):
                        pool.wait_ge(consW, 1)
                    pool.tensor_tensor(e2v[:, :, 1:T + 1], e2[:, :, 1:T + 1], vS[:, :, :],
                                       ALU.mult).then_inc(e2v_done, 1)
                    pool.wait_ge(dE_done, q + 1)
                    pool.wait_ge(e2v_done, q + 1)
                    pool.tensor_tensor(vS[:, :, :], dE[:, :, :], vS[:, :, :], ALU.mult).then_inc(ev_done, 1)
                    pool.wait_ge(qscan, q + 1)
                    pool.tensor_tensor(qS[:, :, 0:T], qS[:, :, 0:T], aA[:, :, :], ALU.mult).then_inc(qm_done, 1)
                    ln_pool(pool, NQ + 2 * q + 1)
                looped(pool, body, NQ)

            @block.vector
            def _(dve):
                dve.memset(flat(kS), NEG).then_inc(consW, 1)
                dve.memset(flat(a2), 0.0).then_inc(consW, 1)
                dve.memset(flat(e2), 0.0).then_inc(consW, 1)
                dve.memset(flat(e2v), 0.0).then_inc(consW, 1)
                dve.memset(flat(wrst), 0.0).then_inc(consW, 1)
                dve.memset(zero16[:, :], 0.0).then_inc(consW, 1)
                dve.wait_ge(consW, 6)
                for c in range(KC):
                    seg_c = wrst[:, 2 * c:2 * c + 2, :]
                    dve.tensor_scalar(seg_c, seg_c, wcol[:, c:c + 1], None, ALU.add).then_inc(consW, 1)
                dve.wait_ge(consW, 6 + KC)
                dve.memset(wrst[:, :, 0:1], NEG).then_inc(consW, 1)
                dve.wait_ge(gate_w, 1)
                dve.tensor_tensor(gate_hl[:, 1, :, :], gate[:, :, :], gate_hl[:, 0, :, :].bitcast(F32),
                                  ALU.subtract).then_inc(gate_w, 1)
                dve.wait_ge(consW, 7 + KC)

                def body(q):
                    if not isinstance(q, int):
                        wait_apart(dve, trX, 2 * q)
                    ln_vector(dve, NQ + 2 * q, 2 * q)
                    dve.wait_ge(kT_in, 2 * q + 2)
                    dve.tensor_tensor_scan(flat(oS), flat(wrst), flat(kS), NEG, ALU.add, ALU.max).then_inc(o_scan, 1)
                    dve.wait_ge(o_scan, q + 1)
                    for c in range(KC):
                        at = slice(2 * c, 2 * c + 2)
                        dve.scalar_tensor_tensor(out=a2[:, at, 1:T + 1], in0=oS[:, at, 0:T], scalar=wcol[:, c:c + 1],
                                                 in1=oS[:, at, 1:T + 1], op0=ALU.add,
                                                 op1=ALU.subtract).then_inc(d2_done, 1)
                    for c in range(KC):
                        at = slice(2 * c, 2 * c + 2)
                        dve.scalar_tensor_tensor(out=dE[:, at, :], in0=kS[:, at, 1:T + 1], scalar=ucol[:, c:c + 1],
                                                 in1=oS[:, at, 0:T], op0=ALU.add,
                                                 op1=ALU.subtract).then_inc(d_done, 1)
                    dve.wait_ge(d_done, 4 * q + 4)
                    dve.tensor_scalar(aA[:, :, :], dE[:, :, :], -1.0, 0.0, ALU.mult, ALU.min).then_inc(amin, 1)
                    dve.wait_ge(amin, q + 1)
                    dve.tensor_scalar(dE[:, :, :], dE[:, :, :], 0.0, None, ALU.min).then_inc(emin, 1)
                    dve.wait_ge(a2_done, q + 1)
                    dve.wait_ge(e2_done, q + 1)
                    wait(dve, den_done, q)
                    dve.tensor_tensor_scan(flat(qS), flat(a2), flat(e2), 0.0, ALU.mult, ALU.add).then_inc(qscan, 1)
                    dve.wait_ge(e2v_done, q + 1)
                    dve.tensor_tensor_scan(flat(pS), flat(a2), flat(e2v), 0.0, ALU.mult, ALU.add).then_inc(pscan, 1)
                    dve.wait_ge(aA_done, q + 1)
                    dve.wait_ge(dE_done, q + 1)
                    dve.wait_ge(qm_done, q + 1)
                    dve.tensor_tensor(dE[:, :, :], qS[:, :, 0:T], dE[:, :, :], ALU.add).then_inc(den_done, 1)
                    dve.wait_ge(pscan, q + 1)
                    dve.tensor_tensor(pS[:, :, 0:T], pS[:, :, 0:T], aA[:, :, :], ALU.mult).then_inc(pm_done, 1)
                    dve.wait_ge(den_done, q + 1)
                    dve.reciprocal(dE[:, :, :], dE[:, :, :]).then_inc(rec_done, 1)
                    dve.wait_ge(ev_done, q + 1)
                    dve.wait_ge(pm_done, q + 1)
                    dve.tensor_tensor(pS[:, :, 0:T], pS[:, :, 0:T], vS[:, :, :], ALU.add).then_inc(num_done, 1)
                    dve.wait_ge(rec_done, q + 1)
                    dve.wait_ge(num_done, q + 1)
                    dve.tensor_tensor(vS[:, :, :], pS[:, :, 0:T], dE[:, :, :], ALU.mult).then_inc(y_done, 1)
                    for j in range(2):
                        dve.wait_ge(trY, 2 * q + j + 1)
                        dve.tensor_tensor(xres[:, 2 * q + j, :], xres[:, 2 * q + j, :], bank[2 + j][:, :],
                                          ALU.add).then_inc(res_done, 1)
                    dve.wait_ge(trK, 2 * q + 2)
                    wait_apart(dve, res_done, 2 * q + 2)
                    ln_vector(dve, NQ + 2 * q + 1, 2 * q)
                    for j in range(2):
                        dve.wait_ge(hiW, 2 * q + j + 1)
                        dve.tensor_tensor(stage[:, j, 1, :], bank[4 + j][:, :], stage[:, j, 0, :].bitcast(F32),
                                          ALU.subtract).then_inc(loW, 1)
                    dve.wait_ge(lg_in, q + 1)
                    dve.reduce_max(mx[:, :], lg[:, :, :], AX.X).then_inc(mx_done, 1)
                    dve.wait_ge(mx_done, q + 1)
                    dve.tensor_tensor(lg[:, :, :], lg[:, :, :], mx[:, :].unsqueeze(2).to_broadcast([P, 2, E]),
                                      ALU.subtract).then_inc(lgs_done, 1)
                    dve.wait_ge(ex16, q + 1)
                    dve.reduce_sum(sm[:, :], pr[:, :, :], AX.X).then_inc(sm_done, 1)
                    dve.wait_ge(sm_done, q + 1)
                    dve.reciprocal(rsm[:, :], sm[:, :]).then_inc(rs_done, 1)
                    dve.wait_ge(rs_done, q + 1)
                    dve.tensor_tensor(pr[:, :, :], pr[:, :, :], rsm[:, :].unsqueeze(2).to_broadcast([P, 2, E]),
                                      ALU.mult).then_inc(pr_done, 1)
                    wait_apart(dve, pr_done, q + 1)
                    for j in range(2):
                        dve.max(m8[:, j, :], pr[:, j, :]).then_inc(m8_done, 1)
                    for j in range(2):
                        dve.wait_ge(m8_done, 2 * q + j + 1)
                        sixth = m8[:, j, TOPK - 1:TOPK]
                        dve.tensor_scalar(gt[:, j, :], pr[:, j, :], sixth, None, ALU.is_gt).then_inc(gt_done, 1)
                        dve.tensor_scalar(eq[:, j, :], pr[:, j, :], sixth, None, ALU.is_equal).then_inc(eq_done, 1)
                    dve.wait_ge(gt_done, 2 * q + 2)
                    dve.reduce_sum(cnt[:, :], gt[:, :, :], AX.X).then_inc(cnt_done, 1)
                    for j in range(2):
                        dve.wait_ge(eq_done, 2 * q + j + 1)
                        dve.tensor_tensor_scan(rank[:, j, :], eq[:, j, :], zero16[:, :], 0.0, ALU.add,
                                               ALU.add).then_inc(rank_done, 1)
                    dve.wait_ge(cnt_done, q + 1)
                    for j in range(2):
                        dve.wait_ge(rank_done, 2 * q + j + 1)
                        dve.tensor_scalar(rank[:, j, :], rank[:, j, :], cnt[:, j:j + 1], TOPK + 0.5, ALU.add,
                                          ALU.is_lt).then_inc(ok_done, 1)
                    dve.wait_ge(ok_done, 2 * q + 2)
                    dve.tensor_tensor(eq[:, :, :], eq[:, :, :], rank[:, :, :], ALU.mult).then_inc(sel_done, 1)
                    dve.wait_ge(sel_done, q + 1)
                    dve.tensor_tensor(eq[:, :, :], eq[:, :, :], gt[:, :, :], ALU.add).then_inc(selg, 1)
                    dve.wait_ge(selg, q + 1)
                    for j in range(2):
                        dve.scalar_tensor_tensor(out=comb[:, 0:E, 2 * q + j], in0=eq[:, j, :], scalar=0.5,
                                                 in1=pr[:, j, :], op0=ALU.mult, op1=ALU.mult).then_inc(comb_done, 1)
                looped(dve, body, NQ)

        g_done, u_done, ht_done, yF_done, tg_done, a1_done, hid_done, hT_hi, hT_lo, added, stored = (
            sem(n) for n in ("g_done", "u_done", "ht_done", "yF_done", "tg_done", "a1_done", "hid_done", "hT_hi",
                             "hT_lo", "added", "stored"))
        fT_in = [sem("fT_in0"), sem("fT_in1")]
        GATE, UP, HT_, YF = bank[0:2], bank[2:4], bank[4], bank[5:7]
        PF = B * (NG + 1)

        def experts(eng, step):
            step(0, 0, 0, 0, 0, True, False, True)

            def group(base, gp, last, split, next_split):
                with eng.Fori(1, B - 2, 2) as b:
                    s = eng.snap(base + b)
                    step(s, 1, b, gp, gp, True, True, split)
                    step(s + 1, 0, b + 1, gp, gp, True, True, split)
                step(base + B - 1, 1, B - 1, gp, gp, True, True, split)
                step(base + B, 0, 0, 1 - gp, gp, not last, True, next_split)

            with eng.Fori(0, NSTEP_F - 4 * B + 1, 2 * B) as base:
                group(base, 0, False, True, True)
                group(base + B, 1, False, True, True)
            group(NSTEP_F - 2 * B, 0, False, True, False)
            group(NSTEP_F - B, 1, True, False, False)

        with nc.Block() as block:
            @block.sync
            def _(sp):
                def step(s, par, b, fw, bw, front, back, split):
                    if not front:
                        return
                    if split:
                        sp.wait_ge(piece_lo, PF + s - 1)
                        sp.dma_start(raw[:, par, :], weights[s + PF]).then_inc(piece_in[par], 16)
                    else:
                        sp.wait_ge(u_done, s - 1)
                    sp.dma_start(xT[:, par, :, :].rearrange("p h n -> p (h n)").bitcast(F32),
                                 xT_ffn[b]).then_inc(fT_in[par], 16)
                experts(sp, step)

            @block.tensor
            def _(pe):
                def first(s, par, fw, half, out, done):
                    n = 0
                    for c in range(KC):
                        for a, w in TERMS:
                            at = c * 2 * I + half * I
                            last = pe.matmul(out[:, 0:I], xT[:, par, a, c * P:(c + 1) * P],
                                             w_hl[w][:, fw, at:at + I], start=n == 0, stop=n == 11)
                            n += 1
                    last.then_inc(done, 1)

                def step(s, par, b, fw, bw, front, back, split):
                    if front:
                        if isinstance(b, int) and b == 0:
                            pe.wait_ge(piece_hi, s + PF)
                            pe.wait_ge(piece_lo, s + PF)
                        pe.wait_ge(fT_in[par], 8 * (s - par) + 16)
                        first(s, par, fw, 0, GATE[par], g_done)
                    if back:
                        pe.wait_ge(hid_done, s)
                        for c in range(IC):
                            last = pe.transpose(HT_[:, c * P:(c + 1) * P], hid[:, c * P:(c + 1) * P], ident[:, :])
                        last.then_inc(ht_done, 1)
                    if front:
                        first(s, par, fw, 1, UP[par], u_done)
                    if back:
                        pe.wait_ge(hT_hi, s)
                        pe.wait_ge(hT_lo, s)
                        n = 0
                        for c in range(IC):
                            for a, w in TERMS:
                                at = W2_AT + c * D
                                last = pe.matmul(YF[1 - par][:, :], hT[:, a, c * P:(c + 1) * P],
                                                 w_hl[w][:, bw, at:at + D], start=n == 0, stop=n == 3 * IC - 1)
                                n += 1
                        last.then_inc(yF_done, 1)
                experts(pe, step)

            @block.scalar
            def _(act):
                def step(s, par, b, fw, bw, front, back, split):
                    if back:
                        act.wait_ge(ht_done, s)
                        act.activation(hT[:, 0, :], HT_[:, 0:IP], ACT.Copy).then_inc(hT_hi, 1)
                    if front:
                        act.wait_ge(g_done, s + 1)
                        wait(act, a1_done, s)
                        act.activation(tg, GATE[par][:, 0:I], ACT.Tanh, scale=0.5).then_inc(tg_done, 1)
                    if front and split:
                        act.wait_ge(u_done, s + 1)
                        piece_act(act, s + PF - par, par, 1 - fw, bass.ds(b * PIECE, PIECE))
                experts(act, step)

            @block.gpsimd
            def _(pool):
                def step(s, par, b, fw, bw, front, back, split):
                    if front and split:
                        piece_pool(pool, s + PF, par, 1 - fw, bass.ds(b * PIECE, PIECE))
                experts(pool, step)
                with pool.Fori(0, B) as b:
                    pool.wait_ge(added, b + NSTEP_F - B + 1)
                    pool.dma_start(out[b], xres[:, b, :]).then_inc(stored, 16)
                pool.wait_ge(stored, 16 * B)

            @block.vector
            def _(dve):
                dve.memset(hid[:, I:IP], 0.0)

                def step(s, par, b, fw, bw, front, back, split):
                    if back:
                        dve.wait_ge(hT_hi, s)
                        dve.tensor_tensor(hT[:, 1, :], HT_[:, 0:IP], hT[:, 0, :].bitcast(F32),
                                          ALU.subtract).then_inc(hT_lo, 1)
                    if front:
                        dve.wait_ge(tg_done, s + 1)
                        dve.scalar_tensor_tensor(out=a1, in0=tg, scalar=1.0, in1=GATE[par][:, 0:I], op0=ALU.add,
                                                 op1=ALU.mult).then_inc(a1_done, 1)
                        dve.wait_ge(u_done, s + 1)
                        dve.wait_ge(a1_done, s + 1)
                        wait(dve, ht_done, s)
                        dve.scalar_tensor_tensor(out=hid[:, 0:I], in0=UP[par][:, 0:I],
                                                 scalar=flat(comb)[:, bass.ds(s, 1)], in1=a1, op0=ALU.mult,
                                                 op1=ALU.mult).then_inc(hid_done, 1)
                    if back:
                        dve.wait_ge(yF_done, s)
                        bb = b - 1 if not isinstance(b, int) else (b - 1) % B
                        dve.tensor_tensor(xres[:, bb, :], xres[:, bb, :], YF[1 - par][:, :],
                                          ALU.add).then_inc(added, 1)
                experts(dve, step)


def kernel(**inputs):
    import numpy as np
    import concourse.bacc as bacc
    from concourse.bass_utils import run_bass_kernel_spmd

    a = {k: np.asarray(v) for k, v in inputs.items()}
    nc = bacc.Bacc("TRN2", target_bir_lowering=False, num_devices=1)

    def chunks(m):
        return m.reshape(-1, P, m.shape[1]).transpose(1, 0, 2).reshape(P, -1)

    groups = []
    for g in range(NG):
        r = slice(g * HG * DH, (g + 1) * HG * DH)
        qk = np.concatenate([a["L0_attn_wq"][r].T, a["L0_attn_wk"][r].T], axis=1)
        used = [chunks(qk), chunks(a["L0_attn_wv"][r].T), chunks(a["L0_attn_wo"][:, r].T)]
        pad = WCOLS - sum(u.shape[1] for u in used)
        groups.append(np.concatenate(used + [np.zeros((P, pad), np.float32)], axis=1))
    ups = [a["L0_ffn_w1"][e] for e in range(E)]
    downs = [a["L0_ffn_w2"][e] for e in range(E)]
    sw1, sw2 = a["L0_ffn_shared_w1"], a["L0_ffn_shared_w2"]
    for h in range(2):
        ups.append(np.concatenate([sw1[h * I:(h + 1) * I], sw1[(2 + h) * I:(3 + h) * I]], axis=0))
        downs.append(sw2[:, h * I:(h + 1) * I])
    for up, down in zip(ups, downs):
        w2 = np.concatenate([down.T, np.zeros((IP - I, D), np.float32)], axis=0)
        groups.append(np.concatenate([chunks(up.T), chunks(w2)], axis=1))
    weights = np.stack(groups).reshape(len(groups), P, B, PIECE).transpose(0, 2, 1, 3).reshape(-1, P, PIECE)

    arrays = {
        "x": a["x"],
        "ctxT": a["ctx_2048"].reshape(NQ, 2, T, KC, P).transpose(0, 4, 3, 1, 2).reshape(NQ, P, KC * 2 * T),
        "weights": weights,
        "qw": a["L0_attn_q_norm_w"],
        "kw": a["L0_attn_k_norm_w"],
        "cos2": np.repeat(a["L0_attn_rope_cos"][:NH], 2, axis=1).reshape(-1),
        "sin2": np.repeat(a["L0_attn_rope_sin"][:NH], 2, axis=1).reshape(-1),
        "wkv_w": a["L0_xattn_w"].reshape(KC, P).T,
        "wkv_u": a["L0_xattn_u"].reshape(KC, P).T,
        "gateT": chunks(a["L0_ffn_gate_w"].T),
    }
    feed, args = {}, []
    for name, v in arrays.items():
        v = np.ascontiguousarray(v)
        feed[f"in_{name}"] = v
        args.append(nc.dram_tensor(f"in_{name}", v.shape, mybir.dt.from_np(v.dtype), kind="ExternalInput").ap())
    args.append(nc.dram_tensor("out_x", (B, T, D), F32, kind="ExternalOutput").ap())
    build(nc, *args)
    r = run_bass_kernel_spmd(nc, [feed], core_ids=[0])
    return r.results[0]["out_x"]
```

```python
from contextlib import ExitStack

import concourse.bass as bass
from concourse import mybir

F32 = mybir.dt.float32
F32R = mybir.dt.float32r
ACT = mybir.ActivationFunctionType
ALU = mybir.AluOpType
AX = mybir.AxisListType

P = 128
B, T, D = 16, 128, 512
NH, DH = 16, 128
E, TOPK, I = 16, 6, 352
NE = E + 2
KC = D // P
HG = 2
NG = NH // HG
IP = 384
IC = IP // P
NQ = B // 2
WCOLS = KC * 2 * I + IC * D
PIECE = WCOLS // B
QK_COLS, V_COLS = KC * 512, KC * 256
W2_AT = KC * 2 * I
NSTEP_B, NSTEP_F = NG * B, NE * B
LN_EPS, RMS_EPS = 1e-5, 1e-6
SCALE, CAP = DH ** -0.5, 50.0
NEG = -1e38
TERMS = ((0, 0), (0, 1), (1, 0))


def wait(eng, sem, count):
    if not isinstance(count, int) or count > 0:
        eng.wait_ge(sem, count)


def build(nc, x, ctxT, weights, qw, kw, cos2, sin2, wkv_w, wkv_u, gateT, out):
    xT_att = nc.dram_tensor("xT_att", (B, P, 2 * D), F32, kind="Internal").ap()
    xT_ffn = nc.dram_tensor("xT_ffn", (B, P, 2 * D), F32, kind="Internal").ap()

    with ExitStack() as ctx:
        def sb(name, shape, dt=F32):
            return ctx.enter_context(nc.sbuf_tensor(name, shape, dt))

        def sem(name):
            return ctx.enter_context(nc.semaphore(name))

        xres = sb("xres", [P, B, D])
        w_hl = [sb("w_hi", [P, 2, WCOLS], F32R), sb("w_lo", [P, 2, WCOLS], F32R)]
        raw = sb("raw", [P, 2, PIECE])
        xT = sb("xT", [P, 2, 2, D], F32R)
        ident = sb("ident", [P, P])
        comb = sb("comb", [P, NE, B])
        expo = sb("expo", [P, 4])
        st6 = sb("st6", [P, 2, 2, 6])
        mv = sb("mv", [P, 2, 2, 2])
        rstd = sb("rstd", [P, 2, 2])
        xn = sb("xn", [P, 2, 2, D])
        stage = sb("stage", [P, 2, 2, D], F32R)

        qkT = sb("qkT", [P, 2, 512], F32R)
        vE = sb("vE", [P, 2, 2, HG, 130], F32R)
        pT = sb("pT", [P, 2, HG, T], F32R)
        oT = sb("oT", [P, 2, HG, T], F32R)
        hT = sb("hT", [P, 2, IP], F32R)
        rope = sb("rope", [P, NH * DH])
        ssq = sb("ssq", [P, 4])
        rr = sb("rr", [P, 4])
        rk = sb("rk", [P, 2, HG])
        rden = sb("rden", [P, HG])
        hold = sb("hold", [P, 32])
        mask = sb("mask", [P, HG, T])
        kscale = sb("kscale", [P, HG])

        def seg(name):
            return sb(name, [P, KC * 2, T + 1])

        kS, oS, a2, e2, e2v, pS, qS, wrst = (seg(n) for n in ("kS", "oS", "a2", "e2", "e2v", "pS", "qS", "wrst"))
        dE, aA, vS = (sb(n, [P, KC * 2, T]) for n in ("dE", "aA", "vS"))
        wcol = sb("wcol", [P, KC])
        ucol = sb("ucol", [P, KC])
        gate = sb("gate", [P, KC, E])
        gate_hl = sb("gate_hl", [P, 2, KC, E], F32R)
        lg, pr, gt, eq, rank, run = (sb(n, [P, B, E]) for n in ("lg", "pr", "gt", "eq", "rank", "run"))
        m8 = sb("m8", [P, B, 8])
        mx, sm, rsm, cnt = (sb(n, [P, B]) for n in ("mx", "sm", "rsm", "cnt"))

        def flat(t):
            return t[:, :, :].rearrange("p a b -> p (a b)")

        sq, rot = flat(a2)[:, 0:512], flat(e2)[:, 0:512]
        th, ex, on = flat(e2v)[:, 0:256], flat(pS)[:, 0:256], flat(qS)[:, 0:256]
        tg, a1, hid = flat(kS)[:, 0:I], flat(oS)[:, 0:I], flat(a2)[:, 0:IP]
        sin_in = [flat(kS)[:, 0:NH * DH // 2], flat(oS)[:, 0:NH * DH // 2]]
        qw_in, kw_in = flat(dE)[:, 0:DH], flat(aA)[:, 0:DH]

        bank = [ctx.enter_context(nc.psum_tensor(f"bank{i}", [P, 512], F32)) for i in range(8)]

        piece_in = [sem("piece_in0"), sem("piece_in1")]
        piece_hi, piece_lo = sem("piece_hi"), sem("piece_lo")
        stats_done, aggr_done, rstd_done, ln_done = sem("stats_done"), sem("aggr_done"), sem("rstd_done"), sem("ln_done")
        var_done = sem("var_done")

        ident_done = sem("ident_done")

        sites = []

        def wait_apart(dve, sem_, count):
            wait(dve, sem_, count)
            if not isinstance(count, int):
                sites.append(sem_)
                dve.tensor_copy(hold[:, len(sites):len(sites) + 1], hold[:, 0:1])

        def ln_stats(dve, k, b, slot):
            for j in range(2):
                dve.bn_stats(st6[:, slot, j, :], xres[:, b + j, :]).then_inc(stats_done, 1)
            for j in range(2):
                wait_apart(dve, stats_done, 2 * k + j + 1)
                dve.bn_aggr(mv[:, slot, j, :], st6[:, slot, j, :]).then_inc(aggr_done, 1)
            dve.wait_ge(aggr_done, 2 * k + 2)
            dve.tensor_scalar(rstd[:, slot, :], mv[:, slot, :, 1], LN_EPS, None, ALU.add).then_inc(var_done, 1)

        def ln_pool(pool, k, slot):
            pool.wait_ge(var_done, k + 1)
            pool.tensor_tensor(rstd[:, slot, :], rstd[:, slot, :], expo[:, 0:2], ALU.pow).then_inc(rstd_done, 1)

        def ln_norm(dve, k, b, slot):
            dve.wait_ge(rstd_done, k + 1)
            for j in range(2):
                dve.tensor_scalar(xn[:, slot, j, :], xres[:, b + j, :], mv[:, slot, j, 0:1],
                                  rstd[:, slot, j:j + 1], ALU.subtract, ALU.mult).then_inc(ln_done, 1)

        def transposes(pe, out, src, done):
            for c in range(KC):
                last = pe.transpose(out[:, c * P:(c + 1) * P], src(c), ident[:, :])
            last.then_inc(done, 1)

        def piece_act(act, even, par, gpar, at):
            act.wait_ge(piece_in[par], 8 * even + 16)
            act.activation(w_hl[0][:, gpar, at], raw[:, par, :], ACT.Copy).then_inc(piece_hi, 1)

        def piece_pool(pool, number, par, gpar, at):
            pool.wait_ge(piece_hi, number + 1)
            pool.tensor_tensor(w_hl[1][:, gpar, at], raw[:, par, :], w_hl[0][:, gpar, at].bitcast(F32),
                               ALU.subtract).then_inc(piece_lo, 1)

        def looped(eng, body, n):
            body(0)
            with eng.Fori(1, n) as q:
                body(q)

        ld_x0, ld_x1, ld_x, ld_c, ld_t, consts = sem("ld_x0"), sem("ld_x1"), sem("ld_x"), sem("ld_c"), sem("ld_t"), sem("consts")
        trA, hiA, loA, stA, tabs = sem("trA"), sem("hiA"), sem("loA"), sem("stA"), sem("tabs")

        def normed_pairs(eng, step):
            step(-1, True, False)
            step(0, True, True)
            with eng.Fori(1, NQ - 1) as q:
                step(q, True, True)
            step(NQ - 1, False, True)

        with nc.Block() as block:
            @block.sync
            def _(sp):
                xt = x.rearrange("b t d -> t b d")
                for at, done in ((slice(0, 2), ld_x0), (slice(2, 4), ld_x1), (slice(4, B), ld_x)):
                    sp.dma_start(xres[:, at, :], xt[:, at, :]).then_inc(done, 16)
                for par in range(2):
                    sp.dma_start(raw[:, par, :], weights[par]).then_inc(piece_in[par], 16)
                half = NH * DH // 2
                for dst, src in ((rope[:, :], cos2), (sin_in[0], sin2[0:half]), (sin_in[1], sin2[half:]),
                                 (qw_in, qw), (kw_in, kw)):
                    sp.dma_start(dst, src.partition_broadcast(P)).then_inc(ld_t, 16)
                for dst, src in ((wcol[:, :], wkv_w), (ucol[:, :], wkv_u), (flat(gate), gateT)):
                    sp.dma_start(dst, src).then_inc(ld_c, 16)

                def store(q):
                    for j in range(2):
                        sp.wait_ge(hiA, 2 * q + j + 1)
                        sp.wait_ge(loA, 2 * q + j + 1)
                        sp.dma_start(xT_att[2 * q + j],
                                     stage[:, j, :, :].rearrange("p h n -> p (h n)").bitcast(F32)).then_inc(stA, 16)

                with sp.Fori(0, NQ - 1) as q:
                    store(q)
                    for par in range(2):
                        sp.wait_ge(piece_lo, 2 * q + par + 1)
                        sp.dma_start(raw[:, par, :], weights[2 * q + 2 + par]).then_inc(piece_in[par], 16)
                store(NQ - 1)
                sp.wait_ge(stA, 16 * B)

            @block.scalar
            def _(act):
                def body(q):
                    for j in range(2):
                        act.wait_ge(trA, 2 * q + j + 1)
                        if j == 0:
                            wait(act, stA, 32 * q)
                        act.activation(stage[:, j, 0, :], bank[j][:, :], ACT.Copy).then_inc(hiA, 1)
                    for par in range(2):
                        piece_act(act, 2 * q, par, 0, bass.ds((2 * q + par) * PIECE, PIECE))
                looped(act, body, NQ)

            @block.gpsimd
            def _(pool):
                pool.memset(expo[:, :], -0.5).then_inc(consts, 1)
                pool.memset(ident[:, :], 0.0).then_inc(consts, 1)
                pool.wait_ge(consts, 2)
                pool.affine_select(out=ident[:, :], in_=ident[:, :], compare_op=ALU.not_equal, fill=1.0, base=0,
                                   pattern=[[-1, P]], channel_multiplier=1).then_inc(ident_done, 1)
                pool.memset(mask[:, :, :], 1.0).then_inc(consts, 1)
                pool.memset(kscale[:, :], SCALE / CAP).then_inc(consts, 1)
                pool.memset(hold[:, :], 0.0).then_inc(consts, 1)
                pool.wait_ge(consts, 5)
                pool.affine_select(out=mask[:, :, :], in_=mask[:, :, :], compare_op=ALU.is_ge, fill=0.0, base=0,
                                   pattern=[[0, HG], [1, T]], channel_multiplier=-1).then_inc(consts, 1)
                pool.memset(comb[:, E:NE, :], 0.5).then_inc(consts, 1)
                for par in range(2):
                    pool.memset(vE[:, par, 0, :, 128:129].bitcast(F32), 1.0).then_inc(consts, 1)
                    pool.memset(vE[:, par, 0, :, 129:130].bitcast(F32), 0.0).then_inc(consts, 1)
                    pool.memset(vE[:, par, 1, :, 128:130].bitcast(F32), 0.0).then_inc(consts, 1)

                def step(q, front, mid):
                    if front:
                        ln_pool(pool, q + 1, 0)
                    if mid:
                        for par in range(2):
                            piece_pool(pool, 2 * q + par, par, 0, bass.ds((2 * q + par) * PIECE, PIECE))
                normed_pairs(pool, step)

            @block.vector
            def _(dve):
                dve.wait_ge(consts, 5)

                def step(q, front, mid):
                    if front:
                        if isinstance(q, int):
                            dve.wait_ge((ld_x0, ld_x1)[q + 1], 16)
                        else:
                            dve.wait_ge(ld_x, 16)
                        ln_stats(dve, q + 1, 2 * q + 2, 0)
                    if mid:
                        for j in range(2):
                            dve.wait_ge(hiA, 2 * q + j + 1)
                            dve.tensor_tensor(stage[:, j, 1, :], bank[j][:, :], stage[:, j, 0, :].bitcast(F32),
                                              ALU.subtract).then_inc(loA, 1)
                    if front:
                        ln_norm(dve, q + 1, 2 * q + 2, 0)
                normed_pairs(dve, step)

            @block.tensor
            def _(pe):
                pe.wait_ge(ident_done, 1)

                def step(q, front, mid):
                    if front:
                        for j in range(2):
                            pe.wait_ge(ln_done, 2 * q + j + 3)
                            if mid:
                                pe.wait_ge(hiA, 2 * q + j + 1)
                                pe.wait_ge(loA, 2 * q + j + 1)
                            transposes(pe, bank[j], lambda c: xn[:, 0, j, c * P:(c + 1) * P], trA)
                normed_pairs(pe, step)

        xT_in = [sem("xT_in0"), sem("xT_in1")]
        (qk_done, s_done, ot_done, v_done, wo_done, pv_done, t_done, sq_done, th_done, ex_done, oT_hi, p_hi,
         v_hi, qkT_hi, k_out, ss_done, oT_lo, p_lo, v_lo, acc_done, rden_done, on_done, qkT_lo,
         mask_done, ms_done, pw_done, rms_done, rot_done) = (sem(n) for n in (
             "qk_done", "s_done", "ot_done", "v_done", "wo_done", "pv_done", "t_done", "sq_done", "th_done",
             "ex_done", "oT_hi", "p_hi", "v_hi", "qkT_hi", "k_out", "ss_done", "oT_lo", "p_lo", "v_lo",
             "acc_done", "rden_done", "on_done", "qkT_lo", "mask_done", "ms_done", "pw_done",
             "rms_done", "rot_done"))
        S_, OT_, V_, Y_, O_, QT_ = bank[2:8]
        heads = lambda ap: ap.rearrange("p (h n) -> p h n", h=HG)

        def attention(eng, step):
            for i in range(4):
                step(i, i % 2, i, 0, 0, 0, True, i > 0, i > 1, i > 2)

            def group(base, gp, last):
                with eng.Fori(4, B - 1, 2) as b:
                    s = eng.snap(base + b)
                    step(s, 0, b, base, gp, gp, True, True, True, True)
                    step(s + 1, 1, b + 1, base, gp, gp, True, True, True, True)
                for i in range(3 if last else 4):
                    step(base + B + i, i % 2, i, base + B, 1 - gp, gp if i < 3 else 1 - gp,
                         not last, not last or i < 1, not last or i < 2, True)

            with eng.Fori(0, NSTEP_B - 4 * B + 1, 2 * B) as base:
                group(base, 0, False)
                group(base + B, 1, False)
            group(NSTEP_B - 2 * B, 0, False)
            group(NSTEP_B - B, 1, True)

        with nc.Block() as block:
            @block.sync
            def _(sp):
                def step(s, par, b, first, fw, bw, front, mid, back, tail):
                    if not front:
                        return
                    wait(sp, v_done, s - 1)
                    sp.dma_start(xT[:, par, :, :].rearrange("p h n -> p (h n)").bitcast(F32),
                                 xT_att[b]).then_inc(xT_in[par], 16)
                    wait(sp, piece_lo, B + s - 1)
                    sp.dma_start(raw[:, par, :], weights[s + B]).then_inc(piece_in[par], 16)
                attention(sp, step)

            @block.tensor
            def _(pe):
                def step(s, par, b, first, fw, bw, front, mid, back, tail):
                    if front:
                        if isinstance(b, int) and b == 0:
                            pe.wait_ge(piece_hi, s + B)
                            pe.wait_ge(piece_lo, s + B)
                        pe.wait_ge(xT_in[par], 8 * (s - par) + 16)
                        n = 0
                        for c in range(KC):
                            for a, w in TERMS:
                                last = pe.matmul(bank[par][:, :], xT[:, par, a, c * P:(c + 1) * P],
                                                 w_hl[w][:, fw, c * 512:(c + 1) * 512],
                                                 start=n == 0, stop=n == 11)
                                n += 1
                        last.then_inc(qk_done, 1)
                    if mid:
                        pe.wait_ge(k_out, s)
                        pe.wait_ge(rot_done, 2 * s)
                        transposes(pe, QT_, lambda c: rot[:, c * P:(c + 1) * P], t_done)
                    if tail:
                        pe.wait_ge(oT_hi, s - 2)
                        pe.wait_ge(oT_lo, s - 2)
                        if not mid:
                            pe.wait_ge(acc_done, s - 3)
                        n = 0
                        for h in range(HG):
                            for a, w in TERMS:
                                at = QK_COLS + V_COLS + h * D
                                last = pe.matmul(Y_[:, :], oT[:, a, h, :], w_hl[w][:, bw, at:at + D],
                                                 start=n == 0, stop=n == 5)
                                n += 1
                        last.then_inc(wo_done, 1)
                    if back:
                        pe.wait_ge(p_hi, s - 1)
                        pe.wait_ge(p_lo, s - 1)
                        pe.wait_ge(v_hi, s - 1)
                        pe.wait_ge(v_lo, s - 1)
                        for h in range(HG):
                            for n, (a, w) in enumerate(TERMS):
                                last = pe.matmul(O_[:, h * 130:(h + 1) * 130], pT[:, a, h, :],
                                                 vE[:, par, w, h, :], start=n == 0, stop=n == 2)
                        last.then_inc(pv_done, 1)
                    if front:
                        wait(pe, v_hi, s)
                        wait(pe, v_lo, s)
                        n = 0
                        for c in range(KC):
                            for a, w in TERMS:
                                at = QK_COLS + c * 256
                                last = pe.matmul(V_[:, 0:256], xT[:, par, a, c * P:(c + 1) * P],
                                                 w_hl[w][:, fw, at:at + 256], start=n == 0, stop=n == 11)
                                n += 1
                        last.then_inc(v_done, 1)
                    if back:
                        pe.wait_ge(on_done, s - 1)
                        for h in range(HG):
                            last = pe.transpose(OT_[:, h * T:(h + 1) * T], on[:, h * DH:(h + 1) * DH], ident[:, :])
                        last.then_inc(ot_done, 1)
                    if mid:
                        pe.wait_ge(qkT_hi, s)
                        pe.wait_ge(qkT_lo, s)
                        wait(pe, th_done, 2 * s - 2)
                        for h in range(HG):
                            for n, (a, w) in enumerate(TERMS):
                                last = pe.matmul(S_[:, h * T:(h + 1) * T], qkT[:, a, (HG + h) * T:(HG + h + 1) * T],
                                                 qkT[:, w, h * T:(h + 1) * T], start=n == 0, stop=n == 2)
                        last.then_inc(s_done, 1)
                attention(pe, step)

            @block.scalar
            def _(act):
                def step(s, par, b, first, fw, bw, front, mid, back, tail):
                    if front:
                        act.wait_ge(qk_done, s + 1)
                        wait(act, ss_done, s)
                        act.activation(sq, bank[par][:, :], ACT.Square).then_inc(sq_done, 1)
                    if mid:
                        act.wait_ge(t_done, s)
                        act.activation(qkT[:, 0, :], QT_[:, :], ACT.Copy).then_inc(qkT_hi, 1)
                    if front:
                        act.activation(rot[:, 256:512], bank[par][:, 256:512], ACT.Copy).then_inc(k_out, 1)
                        piece_act(act, s + B - par, par, 1 - fw, bass.ds(b * PIECE, PIECE))
                        act.wait_ge(v_done, s + 1)
                        act.activation(vE[:, par, 0, :, 0:DH], heads(V_[:, 0:256]), ACT.Copy).then_inc(v_hi, 1)
                    if back:
                        act.wait_ge(ot_done, s - 1)
                        act.activation(oT[:, 0, :, :], heads(OT_[:, 0:256]), ACT.Copy).then_inc(oT_hi, 1)
                    if mid:
                        act.wait_ge(s_done, s)
                        act.wait_ge(rms_done, s)
                        for h in range(HG):
                            act.activation(th[:, h * T:(h + 1) * T], S_[:, h * T:(h + 1) * T], ACT.Tanh,
                                           scale=rk[:, 1 - par, h:h + 1]).then_inc(th_done, 1)
                        act.wait_ge(th_done, 2 * s)
                        wait(act, p_lo, s - 1)
                        act.activation(ex, th, ACT.Exp, scale=CAP).then_inc(ex_done, 1)
                        act.wait_ge(mask_done, s)
                        act.activation(pT[:, 0, :, :], heads(ex), ACT.Copy).then_inc(p_hi, 1)
                attention(act, step)

            @block.vector
            def _(dve):
                def step(s, par, b, first, fw, bw, front, mid, back, tail):
                    if front:
                        dve.wait_ge(sq_done, s + 1)
                        dve.reduce_sum(ssq[:, :], sq.rearrange("p (g n) -> p g n", g=4), AX.X).then_inc(ss_done, 1)
                    if mid:
                        dve.wait_ge(qkT_hi, s)
                        dve.tensor_tensor(qkT[:, 1, :], QT_[:, :], qkT[:, 0, :].bitcast(F32),
                                          ALU.subtract).then_inc(qkT_lo, 1)
                    if front:
                        wait(dve, rms_done, s)
                        dve.wait_ge(ss_done, s + 1)
                        dve.tensor_scalar(rr[:, :], ssq[:, :], 1.0 / DH, RMS_EPS, ALU.mult, ALU.add)\
                            .then_inc(ms_done, 1)
                    if tail:
                        dve.wait_ge(wo_done, s - 2)
                        bb = b - 3 if not isinstance(b, int) else (b - 3) % B
                        dve.tensor_tensor(xres[:, bb, :], xres[:, bb, :], Y_[:, :], ALU.add).then_inc(acc_done, 1)
                    if back:
                        dve.wait_ge(pv_done, s - 1)
                        av = O_[:, 0:HG * 130].rearrange("p (h n) -> p h n", h=HG)
                        dve.reciprocal(rden[:, :], av[:, :, DH]).then_inc(rden_done, 1)
                        dve.wait_ge(rden_done, s - 1)
                        dve.tensor_tensor(heads(on), av[:, :, 0:DH],
                                          rden[:, :].unsqueeze(2).to_broadcast([P, HG, DH]),
                                          ALU.mult).then_inc(on_done, 1)
                    if front:
                        dve.wait_ge(pw_done, s + 1)
                        dve.wait_ge(k_out, s + 1)
                        for h in range(HG):
                            at = first * (HG * DH // B) + h * DH
                            dve.scalar_tensor_tensor(out=rot[:, h * DH:(h + 1) * DH],
                                                     in0=bank[par][:, h * DH:(h + 1) * DH], scalar=rr[:, h:h + 1],
                                                     in1=rope[:, bass.ds(at, DH)], op0=ALU.mult,
                                                     op1=ALU.mult).then_inc(rot_done, 1)
                        dve.wait_ge(v_hi, s + 1)
                        dve.tensor_tensor(vE[:, par, 1, :, 0:DH], heads(V_[:, 0:256]),
                                          vE[:, par, 0, :, 0:DH].bitcast(F32), ALU.subtract).then_inc(v_lo, 1)
                    if back:
                        dve.wait_ge(oT_hi, s - 1)
                        dve.tensor_tensor(oT[:, 1, :, :], heads(OT_[:, 0:256]), oT[:, 0, :, :].bitcast(F32),
                                          ALU.subtract).then_inc(oT_lo, 1)
                    if mid:
                        dve.wait_ge(p_hi, s)
                        dve.tensor_tensor(pT[:, 1, :, :], heads(ex), pT[:, 0, :, :].bitcast(F32),
                                          ALU.subtract).then_inc(p_lo, 1)

                half = NH * DH // 2
                dve.wait_ge(ld_t, 80)
                dve.tensor_tensor(rope[:, :], rope[:, :], rope[:, :], ALU.mult).then_inc(tabs, 1)
                for i in range(2):
                    dve.tensor_tensor(sin_in[i], sin_in[i], sin_in[i], ALU.mult).then_inc(tabs, 1)
                dve.tensor_tensor(qw_in, qw_in, kw_in, ALU.mult).then_inc(tabs, 1)
                dve.wait_ge(tabs, 4)
                for i in range(2):
                    part = rope[:, i * half:(i + 1) * half]
                    dve.tensor_tensor(part, part, sin_in[i], ALU.add).then_inc(tabs, 1)
                dve.wait_ge(tabs, 6)
                all_heads = rope[:, :].rearrange("p (h d) -> p h d", h=NH)
                dve.tensor_tensor(all_heads, all_heads, qw_in.unsqueeze(1).to_broadcast([P, NH, DH]),
                                  ALU.mult).then_inc(tabs, 1)
                attention(dve, step)

            @block.gpsimd
            def _(pool):
                def step(s, par, b, first, fw, bw, front, mid, back, tail):
                    if front:
                        pool.wait_ge(ms_done, s + 1)
                        pool.tensor_tensor(rr[:, :], rr[:, :], expo[:, :], ALU.pow).then_inc(pw_done, 1)
                        wait(pool, th_done, 2 * s - 2)
                        pool.wait_ge(pw_done, s + 1)
                        pool.tensor_tensor(rk[:, par, :], rr[:, HG:4], kscale[:, :], ALU.mult).then_inc(rms_done, 1)
                        piece_pool(pool, s + B, par, 1 - fw, bass.ds(b * PIECE, PIECE))
                    if mid:
                        pool.wait_ge(ex_done, s)
                        pool.tensor_tensor(heads(ex), heads(ex), mask[:, :, :], ALU.mult).then_inc(mask_done, 1)
                attention(pool, step)

        (consW, trK, kT_in, o_scan, d2_done, e2a_done, d_done, emin, amin, a2_done, e2_done, aA_done, dE_done,
         v_in, e2v_done, ev_done, pscan, qscan, pm_done, qm_done, num_done, den_done, rec_done, y_done, trY,
         res_done, trX, hiW, loW, stW, gate_w, lg_done, lg_in) = (
             sem(n) for n in (
                 "consW", "trK", "kT_in", "o_scan", "d2_done", "e2a_done", "d_done", "emin", "amin", "a2_done",
                 "e2_done", "aA_done", "dE_done", "v_in", "e2v_done", "ev_done", "pscan", "qscan", "pm_done",
                 "qm_done", "num_done", "den_done", "rec_done", "y_done", "trY", "res_done", "trX", "hiW",
                 "loW", "stW", "gate_w", "lg_done", "lg_in"))
        cj = lambda t, j: t[:, :, :].rearrange("p (c j) t -> p j c t", j=2)[:, j, :, :]
        LN_W, LN_LAST = NQ, 2 * NQ - 1

        def mixed_pairs(eng, step):
            step(-1, True, False, False)
            step(0, True, True, False)
            with eng.Fori(1, NQ - 1) as q:
                step(q, True, True, True)
            step(NQ - 1, False, True, True)
            step(NQ, False, False, True)

        def call_front(q):
            return LN_W + (max(2 * q + 1, 0) if isinstance(q, int) else 2 * q + 1)

        def call_back(q):
            return LN_W + (min(2 * q, LN_LAST) if isinstance(q, int) else 2 * q)

        with nc.Block() as block:
            @block.sync
            def _(sp):
                def step(q, front, mid, back):
                    if front:
                        wait(sp, trY, 2 * q + 2)
                        sp.dma_start(vS[:, :, :].rearrange("p a t -> p (a t)"), ctxT[q + 1]).then_inc(v_in, 16)
                    if back:
                        for j in range(2):
                            sp.wait_ge(hiW, 2 * q + j - 1)
                            sp.wait_ge(loW, 2 * q + j - 1)
                            sp.dma_start(xT_ffn[2 * q + j - 2],
                                         stage[:, j, :, :].rearrange("p h n -> p (h n)").bitcast(F32))\
                                .then_inc(stW, 16)
                mixed_pairs(sp, step)
                sp.wait_ge(stW, 16 * B)

            @block.tensor
            def _(pe):
                def step(q, front, mid, back):
                    if back:
                        for j in range(2):
                            pe.wait_ge(ln_done, 2 * call_back(q) + j + 1)
                            transposes(pe, bank[4 + j], lambda c: xn[:, 1, j, c * P:(c + 1) * P], trX)
                    if front:
                        for j in range(2):
                            pe.wait_ge(ln_done, 2 * call_front(q) + j + 1)
                            wait(pe, kT_in, 2 * q + 2)
                            transposes(pe, bank[j], lambda c: xn[:, 0, j, c * P:(c + 1) * P], trK)
                    if mid:
                        pe.wait_ge(y_done, q + 1)
                        for j in range(2):
                            transposes(pe, bank[2 + j], lambda c: vS[:, 2 * c + j, :], trY)
                    if back:
                        if isinstance(q, int) and q == 1:
                            pe.wait_ge(gate_w, 2)
                        for j in range(2):
                            pe.wait_ge(hiW, 2 * q + j - 1)
                            pe.wait_ge(loW, 2 * q + j - 1)
                            n = 0
                            for c in range(KC):
                                for a, w in TERMS:
                                    last = pe.matmul(bank[6][:, j * E:(j + 1) * E],
                                                     stage[:, j, a, c * P:(c + 1) * P], gate_hl[:, w, c, :],
                                                     start=n == 0, stop=n == 11)
                                    n += 1
                            last.then_inc(lg_done, 1)
                pe.wait_ge(gate_w, 2)
                mixed_pairs(pe, step)

            @block.scalar
            def _(act):
                act.activation(gate_hl[:, 0, :, :], gate[:, :, :], ACT.Copy).then_inc(gate_w, 1)

                def step(q, front, mid, back):
                    if mid:
                        act.wait_ge(d2_done, 4 * q + 4)
                        act.activation(a2[:, :, 1:T + 1], a2[:, :, 1:T + 1], ACT.Exp).then_inc(a2_done, 1)
                        act.wait_ge(e2a_done, q + 1)
                        act.activation(e2[:, :, 1:T + 1], e2[:, :, 1:T + 1], ACT.Exp).then_inc(e2_done, 1)
                        act.wait_ge(amin, q + 1)
                        act.activation(aA[:, :, :], aA[:, :, :], ACT.Exp).then_inc(aA_done, 1)
                        act.wait_ge(emin, q + 1)
                        act.activation(dE[:, :, :], dE[:, :, :], ACT.Exp).then_inc(dE_done, 1)
                    if back:
                        for j in range(2):
                            act.wait_ge(trX, 2 * q + j - 1)
                            if isinstance(q, int) and q == 1:
                                pass
                            elif j == 0:
                                act.wait_ge(stW, 32 * q - 32)
                                act.wait_ge(lg_done, 2 * q - 2)
                            act.activation(stage[:, j, 0, :], bank[4 + j][:, :], ACT.Copy).then_inc(hiW, 1)
                    if front:
                        for j in range(2):
                            act.wait_ge(trK, 2 * q + j + 3)
                            act.activation(cj(kS, j)[:, :, 1:T + 1],
                                           bank[j][:, :].rearrange("p (c t) -> p c t", c=KC),
                                           ACT.Copy).then_inc(kT_in, 1)
                    if back:
                        act.wait_ge(lg_done, 2 * q)
                        act.activation(lg[:, :, :].rearrange("p b e -> p (b e)")[:, bass.ds((2 * q - 2) * E, 2 * E)],
                                       bank[6][:, 0:2 * E], ACT.Copy).then_inc(lg_in, 1)
                act.wait_ge(consW, 1)
                mixed_pairs(act, step)

            @block.gpsimd
            def _(pool):
                def step(q, front, mid, back):
                    if mid:
                        pool.wait_ge(o_scan, q + 1)
                        pool.tensor_tensor(e2[:, :, 1:T + 1], kS[:, :, 1:T + 1], oS[:, :, 1:T + 1],
                                           ALU.subtract).then_inc(e2a_done, 1)
                    if back:
                        ln_pool(pool, call_back(q), 1)
                    if front:
                        ln_pool(pool, call_front(q), 0)
                    if mid:
                        pool.wait_ge(e2_done, q + 1)
                        pool.wait_ge(v_in, 16 * q + 16)
                        pool.tensor_tensor(e2v[:, :, 1:T + 1], e2[:, :, 1:T + 1], vS[:, :, :],
                                           ALU.mult).then_inc(e2v_done, 1)
                        pool.wait_ge(dE_done, q + 1)
                        pool.wait_ge(e2v_done, q + 1)
                        pool.tensor_tensor(vS[:, :, :], dE[:, :, :], vS[:, :, :], ALU.mult).then_inc(ev_done, 1)
                        pool.wait_ge(qscan, q + 1)
                        pool.tensor_tensor(qS[:, :, 0:T], qS[:, :, 0:T], aA[:, :, :], ALU.mult).then_inc(qm_done, 1)
                pool.wait_ge(consW, 5)
                mixed_pairs(pool, step)

            @block.vector
            def _(dve):
                dve.memset(flat(kS), NEG).then_inc(consW, 1)
                dve.memset(flat(a2), 0.0).then_inc(consW, 1)
                dve.memset(flat(e2), 0.0).then_inc(consW, 1)
                dve.memset(flat(e2v), 0.0).then_inc(consW, 1)
                dve.memset(flat(wrst), 0.0).then_inc(consW, 1)
                dve.wait_ge(consW, 5)
                for c in range(KC):
                    seg_c = wrst[:, 2 * c:2 * c + 2, :]
                    dve.tensor_scalar(seg_c, seg_c, wcol[:, c:c + 1], None, ALU.add).then_inc(consW, 1)
                dve.wait_ge(consW, 5 + KC)
                dve.memset(wrst[:, :, 0:1], NEG).then_inc(consW, 1)
                dve.wait_ge(gate_w, 1)
                dve.tensor_tensor(gate_hl[:, 1, :, :], gate[:, :, :], gate_hl[:, 0, :, :].bitcast(F32),
                                  ALU.subtract).then_inc(gate_w, 1)
                dve.wait_ge(consW, 6 + KC)

                def step(q, front, mid, back):
                    if mid:
                        dve.wait_ge(kT_in, 2 * q + 2)
                        dve.tensor_tensor_scan(flat(oS), flat(wrst), flat(kS), NEG, ALU.add, ALU.max)\
                            .then_inc(o_scan, 1)
                        dve.wait_ge(o_scan, q + 1)
                        for c in range(KC):
                            at = slice(2 * c, 2 * c + 2)
                            dve.scalar_tensor_tensor(out=a2[:, at, 1:T + 1], in0=oS[:, at, 0:T],
                                                     scalar=wcol[:, c:c + 1], in1=oS[:, at, 1:T + 1], op0=ALU.add,
                                                     op1=ALU.subtract).then_inc(d2_done, 1)
                        for c in range(KC):
                            at = slice(2 * c, 2 * c + 2)
                            dve.scalar_tensor_tensor(out=dE[:, at, :], in0=kS[:, at, 1:T + 1],
                                                     scalar=ucol[:, c:c + 1], in1=oS[:, at, 0:T], op0=ALU.add,
                                                     op1=ALU.subtract).then_inc(d_done, 1)
                        dve.wait_ge(d_done, 4 * q + 4)
                        dve.tensor_scalar(aA[:, :, :], dE[:, :, :], -1.0, 0.0, ALU.mult, ALU.min).then_inc(amin, 1)
                        dve.wait_ge(amin, q + 1)
                        dve.tensor_scalar(dE[:, :, :], dE[:, :, :], 0.0, None, ALU.min).then_inc(emin, 1)
                    if back:
                        for j in range(2):
                            dve.wait_ge(trY, 2 * q + j - 1)
                            dve.tensor_tensor(xres[:, 2 * q + j - 2, :], xres[:, 2 * q + j - 2, :],
                                              bank[2 + j][:, :], ALU.add).then_inc(res_done, 1)
                        wait_apart(dve, res_done, 2 * q)
                        ln_stats(dve, call_back(q), 2 * q - 2, 1)
                    if front:
                        ln_stats(dve, call_front(q), 2 * q + 2, 0)
                    if mid:
                        dve.wait_ge(a2_done, q + 1)
                        dve.wait_ge(e2_done, q + 1)
                        dve.tensor_tensor_scan(flat(qS), flat(a2), flat(e2), 0.0, ALU.mult, ALU.add)\
                            .then_inc(qscan, 1)
                        dve.wait_ge(e2v_done, q + 1)
                        dve.tensor_tensor_scan(flat(pS), flat(a2), flat(e2v), 0.0, ALU.mult, ALU.add)\
                            .then_inc(pscan, 1)
                    if back:
                        ln_norm(dve, call_back(q), 2 * q - 2, 1)
                    if front:
                        ln_norm(dve, call_front(q), 2 * q + 2, 0)
                    if mid:
                        dve.wait_ge(aA_done, q + 1)
                        dve.wait_ge(pscan, q + 1)
                        dve.tensor_tensor(pS[:, :, 0:T], pS[:, :, 0:T], aA[:, :, :], ALU.mult).then_inc(pm_done, 1)
                        dve.wait_ge(dE_done, q + 1)
                        dve.wait_ge(ev_done, q + 1)
                        dve.wait_ge(qm_done, q + 1)
                        dve.tensor_tensor(dE[:, :, :], qS[:, :, 0:T], dE[:, :, :], ALU.add).then_inc(den_done, 1)
                        dve.wait_ge(pm_done, q + 1)
                        dve.tensor_tensor(pS[:, :, 0:T], pS[:, :, 0:T], vS[:, :, :], ALU.add).then_inc(num_done, 1)
                        dve.wait_ge(den_done, q + 1)
                        dve.reciprocal(dE[:, :, :], dE[:, :, :]).then_inc(rec_done, 1)
                        dve.wait_ge(rec_done, q + 1)
                        dve.wait_ge(num_done, q + 1)
                        dve.tensor_tensor(vS[:, :, :], pS[:, :, 0:T], dE[:, :, :], ALU.mult).then_inc(y_done, 1)
                    if back:
                        for j in range(2):
                            dve.wait_ge(hiW, 2 * q + j - 1)
                            dve.tensor_tensor(stage[:, j, 1, :], bank[4 + j][:, :], stage[:, j, 0, :].bitcast(F32),
                                              ALU.subtract).then_inc(loW, 1)
                mixed_pairs(dve, step)

        (mx_done, lgs_done, ex16, sm_done, rs_done, pr_done, m8_done, gt_done, eq_done, cnt_done, run_done,
         rank_done, left_done, sel_done, selg_done, comb_done) = (
             sem(n) for n in ("mx_done", "lgs_done", "ex16", "sm_done", "rs_done", "pr_done", "m8_done", "gt_done",
                              "eq_done", "cnt_done", "run_done", "rank_done", "left_done", "sel_done", "selg_done",
                              "comb_done"))

        def routing(dve):
            over = lambda t: t.unsqueeze(2).to_broadcast([P, B, E])
            dve.memset(flat(run), 1.0).then_inc(run_done, 1)
            dve.reduce_max(mx[:, :], lg[:, :, :], AX.X).then_inc(mx_done, 1)
            dve.wait_ge(run_done, 1)
            dve.memset(run[:, :, 0:1], 0.0).then_inc(run_done, 1)
            dve.wait_ge(mx_done, 1)
            dve.tensor_tensor(lg[:, :, :], lg[:, :, :], over(mx[:, :]), ALU.subtract).then_inc(lgs_done, 1)
            dve.wait_ge(ex16, 1)
            dve.reduce_sum(sm[:, :], pr[:, :, :], AX.X).then_inc(sm_done, 1)
            dve.wait_ge(sm_done, 1)
            dve.reciprocal(rsm[:, :], sm[:, :]).then_inc(rs_done, 1)
            dve.wait_ge(rs_done, 1)
            dve.tensor_tensor(pr[:, :, :], pr[:, :, :], over(rsm[:, :]), ALU.mult).then_inc(pr_done, 1)
            dve.wait_ge(pr_done, 1)
            for b in range(B):
                dve.max(m8[:, b, :], pr[:, b, :]).then_inc(m8_done, 1)
            sixth = m8[:, :, TOPK - 1]
            dve.wait_ge(m8_done, B)
            dve.tensor_tensor(gt[:, :, :], pr[:, :, :], over(sixth), ALU.is_gt).then_inc(gt_done, 1)
            dve.tensor_tensor(eq[:, :, :], pr[:, :, :], over(sixth), ALU.is_equal).then_inc(eq_done, 1)
            dve.wait_ge(gt_done, 1)
            dve.reduce_sum(cnt[:, :], gt[:, :, :], AX.X).then_inc(cnt_done, 1)
            dve.wait_ge(eq_done, 1)
            dve.wait_ge(run_done, 2)
            dve.tensor_tensor_scan(flat(rank), flat(run), flat(eq), 0.0, ALU.mult, ALU.add).then_inc(rank_done, 1)
            dve.wait_ge(rank_done, 1)
            dve.wait_ge(cnt_done, 1)
            dve.tensor_tensor(rank[:, :, :], rank[:, :, :], over(cnt[:, :]), ALU.add).then_inc(left_done, 1)
            dve.wait_ge(left_done, 1)
            dve.scalar_tensor_tensor(out=eq[:, :, :], in0=rank[:, :, :], scalar=TOPK + 0.5, in1=eq[:, :, :],
                                     op0=ALU.is_lt, op1=ALU.mult).then_inc(sel_done, 1)
            dve.wait_ge(sel_done, 1)
            dve.tensor_tensor(eq[:, :, :], eq[:, :, :], gt[:, :, :], ALU.add).then_inc(selg_done, 1)
            dve.wait_ge(selg_done, 1)
            dve.scalar_tensor_tensor(out=comb[:, 0:E, :].rearrange("p e b -> p b e"), in0=eq[:, :, :], scalar=0.5,
                                     in1=pr[:, :, :], op0=ALU.mult, op1=ALU.mult).then_inc(comb_done, 1)

        g_done, u_done, ht_done, yF_done, tg_done, a1_done, hid_done, hT_hi, hT_lo, added, stored = (
            sem(n) for n in ("g_done", "u_done", "ht_done", "yF_done", "tg_done", "a1_done", "hid_done", "hT_hi",
                             "hT_lo", "added", "stored"))
        fT_in = [sem("fT_in0"), sem("fT_in1")]
        GATE, UP, HT_, YF = bank[0:2], bank[2:4], bank[4], bank[5:7]
        PF = B * (NG + 1)

        def experts(eng, step):
            step(0, 0, 0, 0, 0, True, False, True)

            def group(base, gp, last, split, next_split):
                with eng.Fori(1, B - 2, 2) as b:
                    s = eng.snap(base + b)
                    step(s, 1, b, gp, gp, True, True, split)
                    step(s + 1, 0, b + 1, gp, gp, True, True, split)
                step(base + B - 1, 1, B - 1, gp, gp, True, True, split)
                step(base + B, 0, 0, 1 - gp, gp, not last, True, next_split)

            with eng.Fori(0, NSTEP_F - 4 * B + 1, 2 * B) as base:
                group(base, 0, False, True, True)
                group(base + B, 1, False, True, True)
            group(NSTEP_F - 2 * B, 0, False, True, False)
            group(NSTEP_F - B, 1, True, False, False)

        with nc.Block() as block:
            @block.sync
            def _(sp):
                def step(s, par, b, fw, bw, front, back, split):
                    if not front:
                        return
                    if split:
                        sp.wait_ge(piece_lo, PF + s - 1)
                        sp.dma_start(raw[:, par, :], weights[s + PF]).then_inc(piece_in[par], 16)
                    else:
                        sp.wait_ge(u_done, s - 1)
                    sp.dma_start(xT[:, par, :, :].rearrange("p h n -> p (h n)").bitcast(F32),
                                 xT_ffn[b]).then_inc(fT_in[par], 16)
                experts(sp, step)

            @block.tensor
            def _(pe):
                def first(s, par, fw, half, out, done):
                    n = 0
                    for c in range(KC):
                        for a, w in TERMS:
                            at = c * 2 * I + half * I
                            last = pe.matmul(out[:, 0:I], xT[:, par, a, c * P:(c + 1) * P],
                                             w_hl[w][:, fw, at:at + I], start=n == 0, stop=n == 11)
                            n += 1
                    last.then_inc(done, 1)

                def step(s, par, b, fw, bw, front, back, split):
                    if front:
                        if isinstance(b, int) and b == 0:
                            pe.wait_ge(piece_hi, s + PF)
                            pe.wait_ge(piece_lo, s + PF)
                        pe.wait_ge(fT_in[par], 8 * (s - par) + 16)
                        first(s, par, fw, 0, GATE[par], g_done)
                    if back:
                        pe.wait_ge(hid_done, s)
                        for c in range(IC):
                            last = pe.transpose(HT_[:, c * P:(c + 1) * P], hid[:, c * P:(c + 1) * P], ident[:, :])
                        last.then_inc(ht_done, 1)
                    if front:
                        first(s, par, fw, 1, UP[par], u_done)
                    if back:
                        pe.wait_ge(hT_hi, s)
                        pe.wait_ge(hT_lo, s)
                        n = 0
                        for c in range(IC):
                            for a, w in TERMS:
                                at = W2_AT + c * D
                                last = pe.matmul(YF[1 - par][:, :], hT[:, a, c * P:(c + 1) * P],
                                                 w_hl[w][:, bw, at:at + D], start=n == 0, stop=n == 3 * IC - 1)
                                n += 1
                        last.then_inc(yF_done, 1)
                experts(pe, step)

            @block.scalar
            def _(act):
                def step(s, par, b, fw, bw, front, back, split):
                    if back:
                        act.wait_ge(ht_done, s)
                        act.activation(hT[:, 0, :], HT_[:, 0:IP], ACT.Copy).then_inc(hT_hi, 1)
                    if front:
                        act.wait_ge(g_done, s + 1)
                        wait(act, a1_done, s)
                        act.activation(tg, GATE[par][:, 0:I], ACT.Tanh, scale=0.5).then_inc(tg_done, 1)
                    if front and split:
                        act.wait_ge(u_done, s + 1)
                        piece_act(act, s + PF - par, par, 1 - fw, bass.ds(b * PIECE, PIECE))
                act.wait_ge(lgs_done, 1)
                act.activation(pr[:, :, :], lg[:, :, :], ACT.Exp).then_inc(ex16, 1)
                experts(act, step)

            @block.gpsimd
            def _(pool):
                def step(s, par, b, fw, bw, front, back, split):
                    if front and split:
                        piece_pool(pool, s + PF, par, 1 - fw, bass.ds(b * PIECE, PIECE))
                experts(pool, step)
                with pool.Fori(0, B) as b:
                    pool.wait_ge(added, b + NSTEP_F - B + 1)
                    pool.dma_start(out[b], xres[:, b, :]).then_inc(stored, 16)
                pool.wait_ge(stored, 16 * B)

            @block.vector
            def _(dve):
                dve.memset(hid[:, I:IP], 0.0)
                routing(dve)

                def step(s, par, b, fw, bw, front, back, split):
                    if back:
                        dve.wait_ge(hT_hi, s)
                        dve.tensor_tensor(hT[:, 1, :], HT_[:, 0:IP], hT[:, 0, :].bitcast(F32),
                                          ALU.subtract).then_inc(hT_lo, 1)
                    if front:
                        dve.wait_ge(tg_done, s + 1)
                        dve.scalar_tensor_tensor(out=a1, in0=tg, scalar=1.0, in1=GATE[par][:, 0:I], op0=ALU.add,
                                                 op1=ALU.mult).then_inc(a1_done, 1)
                        if isinstance(s, int) and s == 0:
                            dve.wait_ge(comb_done, 1)
                        dve.wait_ge(u_done, s + 1)
                        dve.wait_ge(a1_done, s + 1)
                        wait(dve, ht_done, s)
                        dve.scalar_tensor_tensor(out=hid[:, 0:I], in0=UP[par][:, 0:I],
                                                 scalar=flat(comb)[:, bass.ds(s, 1)], in1=a1, op0=ALU.mult,
                                                 op1=ALU.mult).then_inc(hid_done, 1)
                    if back:
                        dve.wait_ge(yF_done, s)
                        bb = b - 1 if not isinstance(b, int) else (b - 1) % B
                        dve.tensor_tensor(xres[:, bb, :], xres[:, bb, :], YF[1 - par][:, :],
                                          ALU.add).then_inc(added, 1)
                experts(dve, step)


def kernel(**inputs):
    import numpy as np
    import concourse.bacc as bacc
    from concourse.bass_utils import run_bass_kernel_spmd

    a = {k: np.asarray(v) for k, v in inputs.items()}
    nc = bacc.Bacc("TRN2", target_bir_lowering=False, num_devices=1)

    def chunks(m):
        return m.reshape(-1, P, m.shape[1]).transpose(1, 0, 2).reshape(P, -1)

    groups = []
    for g in range(NG):
        r = slice(g * HG * DH, (g + 1) * HG * DH)
        qk = np.concatenate([a["L0_attn_wq"][r].T, a["L0_attn_wk"][r].T], axis=1)
        used = [chunks(qk), chunks(a["L0_attn_wv"][r].T), chunks(a["L0_attn_wo"][:, r].T)]
        pad = WCOLS - sum(u.shape[1] for u in used)
        groups.append(np.concatenate(used + [np.zeros((P, pad), np.float32)], axis=1))
    ups = [a["L0_ffn_w1"][e] for e in range(E)]
    downs = [a["L0_ffn_w2"][e] for e in range(E)]
    sw1, sw2 = a["L0_ffn_shared_w1"], a["L0_ffn_shared_w2"]
    for h in range(2):
        ups.append(np.concatenate([sw1[h * I:(h + 1) * I], sw1[(2 + h) * I:(3 + h) * I]], axis=0))
        downs.append(sw2[:, h * I:(h + 1) * I])
    for up, down in zip(ups, downs):
        w2 = np.concatenate([down.T, np.zeros((IP - I, D), np.float32)], axis=0)
        groups.append(np.concatenate([chunks(up.T), chunks(w2)], axis=1))
    weights = np.stack(groups).reshape(len(groups), P, B, PIECE).transpose(0, 2, 1, 3).reshape(-1, P, PIECE)

    arrays = {
        "x": a["x"],
        "ctxT": a["ctx_2048"].reshape(NQ, 2, T, KC, P).transpose(0, 4, 3, 1, 2).reshape(NQ, P, KC * 2 * T),
        "weights": weights,
        "qw": a["L0_attn_q_norm_w"],
        "kw": a["L0_attn_k_norm_w"],
        "cos2": np.repeat(a["L0_attn_rope_cos"][:NH], 2, axis=1).reshape(-1),
        "sin2": np.repeat(a["L0_attn_rope_sin"][:NH], 2, axis=1).reshape(-1),
        "wkv_w": a["L0_xattn_w"].reshape(KC, P).T,
        "wkv_u": a["L0_xattn_u"].reshape(KC, P).T,
        "gateT": chunks(a["L0_ffn_gate_w"].T),
    }
    feed, args = {}, []
    for name, v in arrays.items():
        v = np.ascontiguousarray(v)
        feed[f"in_{name}"] = v
        args.append(nc.dram_tensor(f"in_{name}", v.shape, mybir.dt.from_np(v.dtype), kind="ExternalInput").ap())
    args.append(nc.dram_tensor("out_x", (B, T, D), F32, kind="ExternalOutput").ap())
    build(nc, *args)
    r = run_bass_kernel_spmd(nc, [feed], core_ids=[0])
    return r.results[0]["out_x"]
```

```python
from contextlib import ExitStack

import concourse.bass as bass
from concourse import mybir

F32 = mybir.dt.float32
F32R = mybir.dt.float32r
ACT = mybir.ActivationFunctionType
ALU = mybir.AluOpType
AX = mybir.AxisListType

P = 128
B, T, D = 16, 128, 512
NH, DH = 16, 128
E, TOPK, I = 16, 6, 352
NE = E + 2
KC = D // P
HG = 2
NG = NH // HG
IP = 384
IC = IP // P
NQ = B // 2
WCOLS = KC * 2 * I + IC * D
PIECE = WCOLS // B
QK_COLS, V_COLS = KC * 512, KC * 256
W2_AT = KC * 2 * I
NSTEP_B, NSTEP_F = NG * B, NE * B
LN_EPS, RMS_EPS = 1e-5, 1e-6
SCALE, CAP = DH ** -0.5, 50.0
NEG = -1e38
TERMS = ((0, 0), (0, 1), (1, 0))


def wait(eng, sem, count):
    if not isinstance(count, int) or count > 0:
        eng.wait_ge(sem, count)


def build(nc, x, ctxT, weights, qw, kw, cos, sin, wkv_w, wkv_u, gateT, out):
    xT_att = nc.dram_tensor("xT_att", (B, P, 2 * D), F32, kind="Internal").ap()
    xT_ffn = nc.dram_tensor("xT_ffn", (B, P, 2 * D), F32, kind="Internal").ap()

    with ExitStack() as ctx:
        def sb(name, shape, dt=F32):
            return ctx.enter_context(nc.sbuf_tensor(name, shape, dt))

        def sem(name):
            return ctx.enter_context(nc.semaphore(name))

        xres = sb("xres", [P, B, D])
        w_hl = [sb("w_hi", [P, 2, WCOLS], F32R), sb("w_lo", [P, 2, WCOLS], F32R)]
        raw = sb("raw", [P, 2, PIECE])
        xT = sb("xT", [P, 2, 2, D], F32R)
        ident = sb("ident", [P, P])
        comb = sb("comb", [P, NE, B])
        expo = sb("expo", [P, 4])
        st6 = sb("st6", [P, 2, 2, 6])
        mv = sb("mv", [P, 2, 2, 2])
        rstd = sb("rstd", [P, 2, 2])
        nmean = sb("nmean", [P, 2, 2])
        xn = sb("xn", [P, 2, 2, D])
        stage = sb("stage", [P, 2, 2, D], F32R)

        qkT = sb("qkT", [P, 2, 512], F32R)
        vE = sb("vE", [P, 2, 2, HG, 130], F32R)
        pT = sb("pT", [P, 2, HG, T], F32R)
        oT = sb("oT", [P, 2, HG, T], F32R)
        hT = sb("hT", [P, 2, IP], F32R)
        rope = sb("rope", [P, NH * DH])
        ssq = sb("ssq", [P, 4])
        rr = sb("rr", [P, 4])
        rk = sb("rk", [P, 2, HG])
        rden = sb("rden", [P, HG])
        hold = sb("hold", [P, 32])
        mask = sb("mask", [P, HG, T])
        kscale = sb("kscale", [P, HG])

        def seg(name):
            return sb(name, [P, KC * 2, T + 1])

        kS, oS, a2, e2, e2v, pS, qS, wrst = (seg(n) for n in ("kS", "oS", "a2", "e2", "e2v", "pS", "qS", "wrst"))
        dE, aA, vS = (sb(n, [P, KC * 2, T]) for n in ("dE", "aA", "vS"))
        wcol = sb("wcol", [P, KC])
        ucol = sb("ucol", [P, KC])
        gate = sb("gate", [P, KC, E])
        gate_hl = sb("gate_hl", [P, 2, KC, E], F32R)
        lg, pr, gt, eq, rank, run = (sb(n, [P, B, E]) for n in ("lg", "pr", "gt", "eq", "rank", "run"))
        m8 = sb("m8", [P, B, 8])
        mx, sm, rsm, cnt = (sb(n, [P, B]) for n in ("mx", "sm", "rsm", "cnt"))

        def flat(t):
            return t[:, :, :].rearrange("p a b -> p (a b)")

        sq, rot = flat(a2)[:, 0:512], flat(e2)[:, 0:512]
        th, ex, on = flat(e2v)[:, 0:256], flat(pS)[:, 0:256], flat(qS)[:, 0:256]
        tg, a1, hid = rope[:, 0:I], rope[:, I:2 * I], rope[:, 2 * I:2 * I + IP]
        cos_in, sin_in = flat(kS)[:, 0:NH * DH // 2], flat(oS)[:, 0:NH * DH // 2]
        qw_in, kw_in = flat(dE)[:, 0:DH], flat(aA)[:, 0:DH]

        bank = [ctx.enter_context(nc.psum_tensor(f"bank{i}", [P, 512], F32)) for i in range(8)]

        piece_in = [sem("piece_in0"), sem("piece_in1")]
        piece_hi, piece_lo = sem("piece_hi"), sem("piece_lo")
        stats_done, aggr_done, rstd_done, ln_done = sem("stats_done"), sem("aggr_done"), sem("rstd_done"), sem("ln_done")
        var_done, mean_done, nm_done = sem("var_done"), sem("mean_done"), sem("nm_done")

        ident_done = sem("ident_done")

        sites = []

        def wait_apart(dve, sem_, count):
            wait(dve, sem_, count)
            if not isinstance(count, int):
                sites.append(sem_)
                dve.tensor_copy(hold[:, len(sites):len(sites) + 1], hold[:, 0:1])

        def ln_stats(dve, k, b, slot, used=0):
            for j in range(2):
                dve.bn_stats(st6[:, slot, j, :], xres[:, b + j, :]).then_inc(stats_done, 1)
            for j in range(2):
                wait_apart(dve, stats_done, 2 * k + j + 1)
                dve.bn_aggr(mv[:, slot, j, :], st6[:, slot, j, :]).then_inc(aggr_done, 1)
            dve.wait_ge(aggr_done, 2 * k + 2)
            wait(dve, ln_done, used)
            dve.tensor_scalar(nmean[:, slot, :], mv[:, slot, :, 0], -1.0, None, ALU.mult).then_inc(mean_done, 1)
            dve.tensor_scalar(rstd[:, slot, :], mv[:, slot, :, 1], LN_EPS, None, ALU.add).then_inc(var_done, 1)

        def ln_pool(pool, k, slot):
            pool.wait_ge(var_done, k + 1)
            pool.tensor_tensor(rstd[:, slot, :], rstd[:, slot, :], expo[:, 0:2], ALU.pow).then_inc(rstd_done, 1)
            pool.wait_ge(mean_done, k + 1)
            pool.wait_ge(rstd_done, k + 1)
            pool.tensor_tensor(nmean[:, slot, :], nmean[:, slot, :], rstd[:, slot, :], ALU.mult).then_inc(nm_done, 1)

        def ln_norm(act, k, b, slot):
            act.wait_ge(nm_done, k + 1)
            for j in range(2):
                act.activation(xn[:, slot, j, :], xres[:, b + j, :], ACT.Identity, bias=nmean[:, slot, j:j + 1],
                               scale=rstd[:, slot, j:j + 1]).then_inc(ln_done, 1)

        def transposes(pe, out, src, done):
            for c in range(KC):
                last = pe.transpose(out[:, c * P:(c + 1) * P], src(c), ident[:, :])
            last.then_inc(done, 1)

        def piece_act(act, even, par, gpar, at):
            act.wait_ge(piece_in[par], 8 * even + 16)
            act.activation(w_hl[0][:, gpar, at], raw[:, par, :], ACT.Copy).then_inc(piece_hi, 1)

        def piece_pool(pool, number, par, gpar, at):
            pool.wait_ge(piece_hi, number + 1)
            pool.tensor_tensor(w_hl[1][:, gpar, at], raw[:, par, :], w_hl[0][:, gpar, at].bitcast(F32),
                               ALU.subtract).then_inc(piece_lo, 1)

        def looped(eng, body, n):
            body(0)
            with eng.Fori(1, n) as q:
                body(q)

        ld_x0, ld_x1, ld_x, ld_c, ld_t, consts = sem("ld_x0"), sem("ld_x1"), sem("ld_x"), sem("ld_c"), sem("ld_t"), sem("consts")
        decay, gate_w = sem("decay"), sem("gate_w")
        xT_in = [sem("xT_in0"), sem("xT_in1")]
        trA, hiA, loA, stA, tabs = sem("trA"), sem("hiA"), sem("loA"), sem("stA"), sem("tabs")

        def normed_pairs(eng, step):
            step(-1, 1, True, False)
            step(0, 0, True, True)
            with eng.Fori(1, NQ - 2, 2) as q:
                step(q, 1, True, True)
                step(q + 1, 0, True, True)
            step(NQ - 1, 1, False, True)

        staging = [xT, stage]
        flat_tile = lambda t: t.rearrange("p h n -> p (h n)").bitcast(F32)
        with nc.Block() as block:
            @block.sync
            def _(sp):
                xt = x.rearrange("b t d -> t b d")
                for at, done in ((slice(0, 2), ld_x0), (slice(2, 4), ld_x1), (slice(4, B), ld_x)):
                    sp.dma_start(xres[:, at, :], xt[:, at, :]).then_inc(done, 16)
                for par in range(2):
                    sp.dma_start(raw[:, par, :], weights[par]).then_inc(piece_in[par], 16)
                for dst, src in ((cos_in, cos), (sin_in, sin), (qw_in, qw), (kw_in, kw)):
                    sp.dma_start(dst, src.partition_broadcast(P)).then_inc(ld_t, 16)
                for dst, src in ((wcol[:, :], wkv_w), (ucol[:, :], wkv_u), (flat(gate), gateT)):
                    sp.dma_start(dst, src).then_inc(ld_c, 16)

                def store(q, par):
                    for j in range(2):
                        sp.wait_ge(hiA, 2 * q + j + 1)
                        sp.wait_ge(loA, 2 * q + j + 1)
                        sp.dma_start(xT_att[2 * q + j], flat_tile(staging[par][:, j, :, :])).then_inc(stA, 16)

                def fetch(q):
                    for par in range(2):
                        sp.wait_ge(piece_lo, 2 * q + par + 1)
                        sp.dma_start(raw[:, par, :], weights[2 * q + 2 + par]).then_inc(piece_in[par], 16)

                store(0, 0)
                fetch(0)
                with sp.Fori(1, NQ - 2, 2) as q:
                    store(q, 1)
                    fetch(q)
                    store(q + 1, 0)
                    fetch(q + 1)
                sp.wait_ge(stA, 32 * (NQ - 1))
                for b in range(2):
                    sp.dma_start(flat_tile(xT[:, b, :, :]), xT_att[b]).then_inc(xT_in[b], 16)
                store(NQ - 1, 1)

            @block.scalar
            def _(act):
                def step(q, par, front, mid):
                    if mid:
                        for j in range(2):
                            act.wait_ge(trA, 2 * q + j + 1)
                            if j == 0 and not (isinstance(q, int) and q < 2):
                                act.wait_ge(stA, 32 * q - 32)
                            act.activation(staging[par][:, j, 0, :], bank[j][:, :], ACT.Copy).then_inc(hiA, 1)
                    if front:
                        ln_norm(act, q + 1, 2 * q + 2, 0)
                    if mid:
                        for i in range(2):
                            piece_act(act, 2 * q, i, 0, bass.ds((2 * q + i) * PIECE, PIECE))
                normed_pairs(act, step)
                act.wait_ge(ld_c, 48)
                act.activation(gate_hl[:, 0, :, :], gate[:, :, :], ACT.Copy).then_inc(gate_w, 1)

            @block.gpsimd
            def _(pool):
                pool.memset(expo[:, :], -0.5).then_inc(consts, 1)
                pool.memset(ident[:, :], 0.0).then_inc(consts, 1)
                pool.wait_ge(consts, 2)
                pool.affine_select(out=ident[:, :], in_=ident[:, :], compare_op=ALU.not_equal, fill=1.0, base=0,
                                   pattern=[[-1, P]], channel_multiplier=1).then_inc(ident_done, 1)
                pool.memset(mask[:, :, :], 1.0).then_inc(consts, 1)
                pool.memset(kscale[:, :], SCALE / CAP).then_inc(consts, 1)
                pool.memset(hold[:, :], 0.0).then_inc(consts, 1)
                pool.wait_ge(consts, 5)
                pool.affine_select(out=mask[:, :, :], in_=mask[:, :, :], compare_op=ALU.is_ge, fill=0.0, base=0,
                                   pattern=[[0, HG], [1, T]], channel_multiplier=-1).then_inc(consts, 1)
                pool.memset(comb[:, 0:NE - E, :], 0.5).then_inc(consts, 1)
                for par in range(2):
                    pool.memset(vE[:, par, 0, :, 128:129].bitcast(F32), 1.0).then_inc(consts, 1)
                    pool.memset(vE[:, par, 0, :, 129:130].bitcast(F32), 0.0).then_inc(consts, 1)
                    pool.memset(vE[:, par, 1, :, 128:130].bitcast(F32), 0.0).then_inc(consts, 1)

                def step(q, par, front, mid):
                    if front:
                        ln_pool(pool, q + 1, 0)
                    if mid:
                        for i in range(2):
                            piece_pool(pool, 2 * q + i, i, 0, bass.ds((2 * q + i) * PIECE, PIECE))
                normed_pairs(pool, step)

            @block.vector
            def _(dve):
                dve.wait_ge(consts, 5)

                def step(q, par, front, mid):
                    if front:
                        if isinstance(q, int):
                            dve.wait_ge((ld_x0, ld_x1)[q + 1], 16)
                        else:
                            dve.wait_ge(ld_x, 16)
                        ln_stats(dve, q + 1, 2 * q + 2, 0, used=2 * q + 2)
                    if mid:
                        for j in range(2):
                            dve.wait_ge(hiA, 2 * q + j + 1)
                            dve.tensor_tensor(staging[par][:, j, 1, :], bank[j][:, :],
                                              staging[par][:, j, 0, :].bitcast(F32), ALU.subtract).then_inc(loA, 1)
                normed_pairs(dve, step)
                dve.memset(flat(wrst), 0.0).then_inc(decay, 1)
                dve.wait_ge(decay, 1)
                dve.wait_ge(ld_c, 48)
                for c in range(KC):
                    seg_c = wrst[:, 2 * c:2 * c + 2, :]
                    dve.tensor_scalar(seg_c, seg_c, wcol[:, c:c + 1], None, ALU.add).then_inc(decay, 1)
                dve.wait_ge(decay, 1 + KC)
                dve.memset(wrst[:, :, 0:1], NEG).then_inc(decay, 1)
                dve.wait_ge(gate_w, 1)
                dve.tensor_tensor(gate_hl[:, 1, :, :], gate[:, :, :], gate_hl[:, 0, :, :].bitcast(F32),
                                  ALU.subtract).then_inc(gate_w, 1)

            @block.tensor
            def _(pe):
                pe.wait_ge(ident_done, 1)

                def step(q, par, front, mid):
                    if front:
                        for j in range(2):
                            pe.wait_ge(ln_done, 2 * q + j + 3)
                            if mid:
                                pe.wait_ge(hiA, 2 * q + j + 1)
                                pe.wait_ge(loA, 2 * q + j + 1)
                            transposes(pe, bank[j], lambda c: xn[:, 0, j, c * P:(c + 1) * P], trA)
                normed_pairs(pe, step)

        (qk_done, s_done, ot_done, v_done, wo_done, pv_done, t_done, sq_done, th_done, ex_done, oT_hi, p_hi,
         v_hi, qkT_hi, k_out, ss_done, oT_lo, p_lo, v_lo, acc_done, rden_done, on_done, qkT_lo,
         mask_done, ms_done, pw_done, rms_done, rot_done) = (sem(n) for n in (
             "qk_done", "s_done", "ot_done", "v_done", "wo_done", "pv_done", "t_done", "sq_done", "th_done",
             "ex_done", "oT_hi", "p_hi", "v_hi", "qkT_hi", "k_out", "ss_done", "oT_lo", "p_lo", "v_lo",
             "acc_done", "rden_done", "on_done", "qkT_lo", "mask_done", "ms_done", "pw_done",
             "rms_done", "rot_done"))
        S_, OT_, V_, Y_, O_, QT_ = bank[2:8]
        v_in = sem("v_in")
        LN_W, LN_LAST = NQ, 2 * NQ - 1
        heads = lambda ap: ap.rearrange("p (h n) -> p h n", h=HG)

        def attention(eng, step):
            for i in range(4):
                step(i, i % 2, i, 0, 0, 0, True, i > 0, i > 1, i > 2)

            def group(base, gp, last):
                with eng.Fori(4, B - 1, 2) as b:
                    s = eng.snap(base + b)
                    step(s, 0, b, base, gp, gp, True, True, True, True)
                    step(s + 1, 1, b + 1, base, gp, gp, True, True, True, True)
                for i in range(3 if last else 4):
                    step(base + B + i, i % 2, i, base + B, 1 - gp, gp if i < 3 else 1 - gp,
                         not last, not last or i < 1, not last or i < 2, True)

            with eng.Fori(0, NSTEP_B - 4 * B + 1, 2 * B) as base:
                group(base, 0, False)
                group(base + B, 1, False)
            group(NSTEP_B - 2 * B, 0, False)
            group(NSTEP_B - B, 1, True)

        with nc.Block() as block:
            @block.sync
            def _(sp):
                def step(s, par, b, first, fw, bw, front, mid, back, tail):
                    if not front:
                        return
                    if isinstance(s, int) and s == 2:
                        sp.wait_ge(stA, 16 * B)
                    if not (isinstance(s, int) and s < 2):
                        sp.wait_ge(v_done, s - 1)
                        sp.dma_start(flat_tile(xT[:, par, :, :]), xT_att[b]).then_inc(xT_in[par], 16)
                    wait(sp, piece_lo, B + s - 1)
                    sp.dma_start(raw[:, par, :], weights[s + B]).then_inc(piece_in[par], 16)
                attention(sp, step)
                sp.dma_start(vS[:, :, :].rearrange("p a t -> p (a t)"), ctxT[0]).then_inc(v_in, 16)

            @block.tensor
            def _(pe):
                def step(s, par, b, first, fw, bw, front, mid, back, tail):
                    if front:
                        if isinstance(b, int) and b == 0:
                            pe.wait_ge(piece_hi, s + B)
                            pe.wait_ge(piece_lo, s + B)
                        pe.wait_ge(xT_in[par], 8 * (s - par) + 16)
                        n = 0
                        for c in range(KC):
                            for a, w in TERMS:
                                last = pe.matmul(bank[par][:, :], xT[:, par, a, c * P:(c + 1) * P],
                                                 w_hl[w][:, fw, c * 512:(c + 1) * 512],
                                                 start=n == 0, stop=n == 11)
                                n += 1
                        last.then_inc(qk_done, 1)
                    if mid:
                        pe.wait_ge(k_out, s)
                        pe.wait_ge(rot_done, 2 * s)
                        transposes(pe, QT_, lambda c: rot[:, c * P:(c + 1) * P], t_done)
                    if tail:
                        pe.wait_ge(oT_hi, s - 2)
                        pe.wait_ge(oT_lo, s - 2)
                        if not mid:
                            pe.wait_ge(acc_done, s - 3)
                        n = 0
                        for h in range(HG):
                            for a, w in TERMS:
                                at = QK_COLS + V_COLS + h * D
                                last = pe.matmul(Y_[:, :], oT[:, a, h, :], w_hl[w][:, bw, at:at + D],
                                                 start=n == 0, stop=n == 5)
                                n += 1
                        last.then_inc(wo_done, 1)
                    if back:
                        pe.wait_ge(p_hi, s - 1)
                        pe.wait_ge(p_lo, s - 1)
                        pe.wait_ge(v_hi, s - 1)
                        pe.wait_ge(v_lo, s - 1)
                        for h in range(HG):
                            for n, (a, w) in enumerate(TERMS):
                                last = pe.matmul(O_[:, h * 130:(h + 1) * 130], pT[:, a, h, :],
                                                 vE[:, par, w, h, :], start=n == 0, stop=n == 2)
                        last.then_inc(pv_done, 1)
                    if front:
                        wait(pe, v_hi, s)
                        wait(pe, v_lo, s)
                        n = 0
                        for c in range(KC):
                            for a, w in TERMS:
                                at = QK_COLS + c * 256
                                last = pe.matmul(V_[:, 0:256], xT[:, par, a, c * P:(c + 1) * P],
                                                 w_hl[w][:, fw, at:at + 256], start=n == 0, stop=n == 11)
                                n += 1
                        last.then_inc(v_done, 1)
                    if back:
                        pe.wait_ge(on_done, s - 1)
                        for h in range(HG):
                            last = pe.transpose(OT_[:, h * T:(h + 1) * T], on[:, h * DH:(h + 1) * DH], ident[:, :])
                        last.then_inc(ot_done, 1)
                    if mid:
                        pe.wait_ge(qkT_hi, s)
                        pe.wait_ge(qkT_lo, s)
                        wait(pe, th_done, 2 * s - 2)
                        for h in range(HG):
                            for n, (a, w) in enumerate(TERMS):
                                last = pe.matmul(S_[:, h * T:(h + 1) * T], qkT[:, a, (HG + h) * T:(HG + h + 1) * T],
                                                 qkT[:, w, h * T:(h + 1) * T], start=n == 0, stop=n == 2)
                        last.then_inc(s_done, 1)
                attention(pe, step)

            @block.scalar
            def _(act):
                def step(s, par, b, first, fw, bw, front, mid, back, tail):
                    if front:
                        act.wait_ge(qk_done, s + 1)
                        wait(act, ss_done, s)
                        act.activation(sq, bank[par][:, :], ACT.Square).then_inc(sq_done, 1)
                    if mid:
                        act.wait_ge(t_done, s)
                        act.activation(qkT[:, 0, :], QT_[:, :], ACT.Copy).then_inc(qkT_hi, 1)
                    if front:
                        act.activation(rot[:, 256:512], bank[par][:, 256:512], ACT.Copy).then_inc(k_out, 1)
                        piece_act(act, s + B - par, par, 1 - fw, bass.ds(b * PIECE, PIECE))
                        act.wait_ge(v_done, s + 1)
                        act.activation(vE[:, par, 0, :, 0:DH], heads(V_[:, 0:256]), ACT.Copy).then_inc(v_hi, 1)
                    if back:
                        act.wait_ge(ot_done, s - 1)
                        act.activation(oT[:, 0, :, :], heads(OT_[:, 0:256]), ACT.Copy).then_inc(oT_hi, 1)
                    if mid:
                        act.wait_ge(s_done, s)
                        act.wait_ge(rms_done, s)
                        for h in range(HG):
                            act.activation(th[:, h * T:(h + 1) * T], S_[:, h * T:(h + 1) * T], ACT.Tanh,
                                           scale=rk[:, 1 - par, h:h + 1]).then_inc(th_done, 1)
                        act.wait_ge(th_done, 2 * s)
                        wait(act, p_lo, s - 1)
                        act.activation(ex, th, ACT.Exp, scale=CAP).then_inc(ex_done, 1)
                        act.wait_ge(mask_done, s)
                        act.activation(pT[:, 0, :, :], heads(ex), ACT.Copy).then_inc(p_hi, 1)
                attention(act, step)
                ln_norm(act, LN_W, 0, 0)

            @block.vector
            def _(dve):
                def step(s, par, b, first, fw, bw, front, mid, back, tail):
                    if isinstance(s, int) and s == NSTEP_B + 1:
                        dve.wait_ge(acc_done, NSTEP_B - 3)
                        ln_stats(dve, LN_W, 0, 0)
                    if front:
                        dve.wait_ge(sq_done, s + 1)
                        dve.reduce_sum(ssq[:, :], sq.rearrange("p (g n) -> p g n", g=4), AX.X).then_inc(ss_done, 1)
                    if mid:
                        dve.wait_ge(qkT_hi, s)
                        dve.tensor_tensor(qkT[:, 1, :], QT_[:, :], qkT[:, 0, :].bitcast(F32),
                                          ALU.subtract).then_inc(qkT_lo, 1)
                    if front:
                        wait(dve, rms_done, s)
                        dve.wait_ge(ss_done, s + 1)
                        dve.tensor_scalar(rr[:, :], ssq[:, :], 1.0 / DH, RMS_EPS, ALU.mult, ALU.add)\
                            .then_inc(ms_done, 1)
                    if tail:
                        dve.wait_ge(wo_done, s - 2)
                        bb = b - 3 if not isinstance(b, int) else (b - 3) % B
                        dve.tensor_tensor(xres[:, bb, :], xres[:, bb, :], Y_[:, :], ALU.add).then_inc(acc_done, 1)
                    if back:
                        dve.wait_ge(pv_done, s - 1)
                        av = O_[:, 0:HG * 130].rearrange("p (h n) -> p h n", h=HG)
                        dve.reciprocal(rden[:, :], av[:, :, DH]).then_inc(rden_done, 1)
                        dve.wait_ge(rden_done, s - 1)
                        dve.tensor_tensor(heads(on), av[:, :, 0:DH],
                                          rden[:, :].unsqueeze(2).to_broadcast([P, HG, DH]),
                                          ALU.mult).then_inc(on_done, 1)
                    if front:
                        dve.wait_ge(pw_done, s + 1)
                        dve.wait_ge(k_out, s + 1)
                        for h in range(HG):
                            at = first * (HG * DH // B) + h * DH
                            dve.scalar_tensor_tensor(out=rot[:, h * DH:(h + 1) * DH],
                                                     in0=bank[par][:, h * DH:(h + 1) * DH], scalar=rr[:, h:h + 1],
                                                     in1=rope[:, bass.ds(at, DH)], op0=ALU.mult,
                                                     op1=ALU.mult).then_inc(rot_done, 1)
                        dve.wait_ge(v_hi, s + 1)
                        dve.tensor_tensor(vE[:, par, 1, :, 0:DH], heads(V_[:, 0:256]),
                                          vE[:, par, 0, :, 0:DH].bitcast(F32), ALU.subtract).then_inc(v_lo, 1)
                    if back:
                        dve.wait_ge(oT_hi, s - 1)
                        dve.tensor_tensor(oT[:, 1, :, :], heads(OT_[:, 0:256]), oT[:, 0, :, :].bitcast(F32),
                                          ALU.subtract).then_inc(oT_lo, 1)
                    if mid:
                        dve.wait_ge(p_hi, s)
                        dve.tensor_tensor(pT[:, 1, :, :], heads(ex), pT[:, 0, :, :].bitcast(F32),
                                          ALU.subtract).then_inc(p_lo, 1)

                dve.wait_ge(ld_t, 64)
                dve.tensor_tensor(cos_in, cos_in, cos_in, ALU.mult).then_inc(tabs, 1)
                dve.tensor_tensor(sin_in, sin_in, sin_in, ALU.mult).then_inc(tabs, 1)
                dve.tensor_tensor(qw_in, qw_in, kw_in, ALU.mult).then_inc(tabs, 1)
                dve.wait_ge(tabs, 3)
                dve.tensor_tensor(cos_in, cos_in, sin_in, ALU.add).then_inc(tabs, 1)
                dve.wait_ge(tabs, 4)
                squares = cos_in.rearrange("p (h i) -> p h i", h=NH)
                norms = qw_in.rearrange("p (i two) -> p i two", two=2)
                factors = rope[:, :].rearrange("p (h i two) -> p h i two", h=NH, two=2)
                for two in range(2):
                    dve.tensor_tensor(factors[:, :, :, two], squares,
                                      norms[:, :, two].unsqueeze(1).to_broadcast([P, NH, DH // 2]),
                                      ALU.mult).then_inc(tabs, 1)
                dve.wait_ge(tabs, 6)
                attention(dve, step)

            @block.gpsimd
            def _(pool):
                def step(s, par, b, first, fw, bw, front, mid, back, tail):
                    if front:
                        pool.wait_ge(ms_done, s + 1)
                        pool.tensor_tensor(rr[:, :], rr[:, :], expo[:, :], ALU.pow).then_inc(pw_done, 1)
                        wait(pool, th_done, 2 * s - 2)
                        pool.wait_ge(pw_done, s + 1)
                        pool.tensor_tensor(rk[:, par, :], rr[:, HG:4], kscale[:, :], ALU.mult).then_inc(rms_done, 1)
                        piece_pool(pool, s + B, par, 1 - fw, bass.ds(b * PIECE, PIECE))
                    if mid:
                        pool.wait_ge(ex_done, s)
                        pool.tensor_tensor(heads(ex), heads(ex), mask[:, :, :], ALU.mult).then_inc(mask_done, 1)
                attention(pool, step)
                ln_pool(pool, LN_W, 0)

        (consW, trK, kT_in, o_scan, d2_done, e2a_done, d_done, emin, amin, a2_done, e2_done, aA_done, dE_done,
         e2v_done, ev_done, pscan, qscan, pm_done, qm_done, num_done, den_done, rec_done, y_done, trY,
         res_done, trX, hiW, loW, stW, lg_done, lg_in) = (
             sem(n) for n in (
                 "consW", "trK", "kT_in", "o_scan", "d2_done", "e2a_done", "d_done", "emin", "amin", "a2_done",
                 "e2_done", "aA_done", "dE_done", "e2v_done", "ev_done", "pscan", "qscan", "pm_done",
                 "qm_done", "num_done", "den_done", "rec_done", "y_done", "trY", "res_done", "trX", "hiW",
                 "loW", "stW", "lg_done", "lg_in"))
        fT_in = [sem("fT_in0"), sem("fT_in1")]
        g_done, u_done, ht_done, yF_done, tg_done, a1_done, hid_done, hT_hi, hT_lo, added, stored = (
            sem(n) for n in ("g_done", "u_done", "ht_done", "yF_done", "tg_done", "a1_done", "hid_done", "hT_hi",
                             "hT_lo", "added", "stored"))
        PF = B * (NG + 1)
        G0_, U0_, Y0_ = bank[2], bank[3], bank[7]
        cj = lambda t, j: t[:, :, :].rearrange("p (c j) t -> p j c t", j=2)[:, j, :, :]

        def first(pe, par, fw, half, out, done):
            n = 0
            for c in range(KC):
                for a, w in TERMS:
                    at = c * 2 * I + half * I
                    last = pe.matmul(out[:, 0:I], xT[:, par, a, c * P:(c + 1) * P],
                                     w_hl[w][:, fw, at:at + I], start=n == 0, stop=n == 11)
                    n += 1
            last.then_inc(done, 1)

        def second(pe, bw, out):
            n = 0
            for c in range(IC):
                for a, w in TERMS:
                    at = W2_AT + c * D
                    last = pe.matmul(out[:, :], hT[:, a, c * P:(c + 1) * P], w_hl[w][:, bw, at:at + D],
                                     start=n == 0, stop=n == 3 * IC - 1)
                    n += 1
            last.then_inc(yF_done, 1)

        def hidden_transposes(pe, out):
            for c in range(IC):
                last = pe.transpose(out[:, c * P:(c + 1) * P], hid[:, c * P:(c + 1) * P], ident[:, :])
            last.then_inc(ht_done, 1)

        def gate_out(act, src):
            act.activation(tg, src[:, 0:I], ACT.Tanh, scale=0.5).then_inc(tg_done, 1)

        def hidden_hi(act, src):
            act.activation(hT[:, 0, :], src[:, 0:IP], ACT.Copy).then_inc(hT_hi, 1)

        def hidden_lo(dve, src):
            dve.tensor_tensor(hT[:, 1, :], src[:, 0:IP], hT[:, 0, :].bitcast(F32), ALU.subtract).then_inc(hT_lo, 1)

        def gated(dve, src):
            dve.scalar_tensor_tensor(out=a1, in0=tg, scalar=1.0, in1=src[:, 0:I], op0=ALU.add,
                                     op1=ALU.mult).then_inc(a1_done, 1)

        def hidden(dve, s, src):
            dve.scalar_tensor_tensor(out=hid[:, 0:I], in0=src[:, 0:I], scalar=flat(comb)[:, bass.ds(s, 1)],
                                     in1=a1, op0=ALU.mult, op1=ALU.mult).then_inc(hid_done, 1)

        def add_up(dve, tile, src):
            dve.tensor_tensor(xres[:, tile, :], xres[:, tile, :], src[:, :], ALU.add).then_inc(added, 1)

        def mixed_pairs(eng, step):
            step(-1, True, False, False, False, False, False)
            step(0, True, True, False, False, False, False)
            step(1, True, True, True, False, False, False)
            step(2, True, True, True, True, True, False)
            with eng.Fori(3, NQ - 1) as q:
                step(q, True, True, True, True, True, True)
            step(NQ - 1, False, True, True, True, True, True)
            step(NQ, False, False, True, True, False, True)
            step(NQ + 1, False, False, False, True, False, False)

        EARLY = 2 * (NQ - 2)

        def call_front(q):
            return LN_W + (max(2 * q + 1, 0) if isinstance(q, int) else 2 * q + 1)

        def call_back(q):
            return LN_W + (min(2 * q, LN_LAST) if isinstance(q, int) else 2 * q)

        with nc.Block() as block:
            @block.sync
            def _(sp):
                def step(q, front, mid, back, routed, tail, rest):
                    if tail:
                        sp.wait_ge(stW, 32 * q - 32)
                        for i in range(2):
                            s = 2 * q - 4 + i
                            sp.wait_ge(piece_lo, PF + s - 1)
                            sp.dma_start(raw[:, i, :], weights[s + PF]).then_inc(piece_in[i], 16)
                            wait(sp, u_done, s - 1)
                            sp.dma_start(flat_tile(xT[:, i, :, :]), xT_ffn[s]).then_inc(fT_in[i], 16)
                    if isinstance(q, int) and q == NQ:
                        sp.wait_ge(stW, 32 * (NQ - 1))
                        sp.wait_ge(u_done, EARLY - 1)
                        sp.dma_start(flat_tile(xT[:, 0, :, :]), xT_ffn[EARLY]).then_inc(fT_in[0], 16)
                    if front and mid:
                        sp.wait_ge(trY, 2 * q + 2)
                        sp.dma_start(vS[:, :, :].rearrange("p a t -> p (a t)"), ctxT[q + 1]).then_inc(v_in, 16)
                    if back:
                        for j in range(2):
                            sp.wait_ge(hiW, 2 * q + j - 1)
                            sp.wait_ge(loW, 2 * q + j - 1)
                            sp.dma_start(xT_ffn[2 * q + j - 2],
                                         stage[:, j, :, :].rearrange("p h n -> p (h n)").bitcast(F32))\
                                .then_inc(stW, 16)
                mixed_pairs(sp, step)

            @block.tensor
            def _(pe):
                def step(q, front, mid, back, routed, tail, rest):
                    s = 2 * q - 4
                    if rest:
                        pe.wait_ge(hid_done, s)
                        hidden_transposes(pe, G0_)
                    if back:
                        for j in range(2):
                            pe.wait_ge(ln_done, 2 * call_back(q) + j + 1)
                            transposes(pe, bank[4 + j], lambda c: xn[:, 1, j, c * P:(c + 1) * P], trX)
                    if front:
                        for j in range(2):
                            pe.wait_ge(ln_done, 2 * call_front(q) + j + 1)
                            transposes(pe, bank[j], lambda c: xn[:, 0, j, c * P:(c + 1) * P], trK)
                    if rest:
                        pe.wait_ge(hT_hi, s)
                        pe.wait_ge(hT_lo, s)
                        pe.wait_ge(added, s - 1)
                        second(pe, 0, Y0_)
                    if tail:
                        if isinstance(q, int) and q == 2:
                            pe.wait_ge(piece_hi, PF)
                            pe.wait_ge(piece_lo, PF)
                        pe.wait_ge(fT_in[0], 8 * s + 16)
                        first(pe, 0, 0, 0, G0_, g_done)
                        first(pe, 0, 0, 1, U0_, u_done)
                        pe.wait_ge(hid_done, s + 1)
                        hidden_transposes(pe, G0_)
                        pe.wait_ge(hT_hi, s + 1)
                        pe.wait_ge(hT_lo, s + 1)
                        wait(pe, added, s)
                        second(pe, 0, Y0_)
                    if mid:
                        pe.wait_ge(y_done, q + 1)
                        if front:
                            pe.wait_ge(kT_in, 2 * q + 4)
                        for j in range(2):
                            transposes(pe, bank[j], lambda c: vS[:, 2 * c + j, :], trY)
                    if tail:
                        pe.wait_ge(fT_in[1], 8 * s + 16)
                        first(pe, 1, 0, 0, G0_, g_done)
                        first(pe, 1, 0, 1, U0_, u_done)
                    if back:
                        for j in range(2):
                            pe.wait_ge(hiW, 2 * q + j - 1)
                            pe.wait_ge(loW, 2 * q + j - 1)
                            n = 0
                            for c in range(KC):
                                for a, w in TERMS:
                                    last = pe.matmul(bank[6][:, j * E:(j + 1) * E],
                                                     stage[:, j, a, c * P:(c + 1) * P], gate_hl[:, w, c, :],
                                                     start=n == 0, stop=n == 11)
                                    n += 1
                            last.then_inc(lg_done, 1)
                mixed_pairs(pe, step)

            @block.scalar
            def _(act):
                def step(q, front, mid, back, routed, tail, rest):
                    if mid:
                        act.wait_ge(d_done, 4 * q + 4)
                        wait(act, pm_done, q)
                        act.activation(aA[:, :, :], dE[:, :, :], ACT.Relu).then_inc(amin, 1)
                        act.wait_ge(amin, q + 1)
                        act.activation(dE[:, :, :], dE[:, :, :], ACT.Relu, scale=-1.0).then_inc(emin, 1)
                    s = 2 * q - 4
                    if rest:
                        act.wait_ge(g_done, s)
                        act.wait_ge(a1_done, s - 1)
                        gate_out(act, G0_)
                    if mid:
                        act.wait_ge(d2_done, q + 1)
                        for c in range(KC):
                            at = slice(2 * c, 2 * c + 2)
                            act.activation(a2[:, at, 1:T + 1], a2[:, at, 1:T + 1], ACT.Exp,
                                           bias=wcol[:, c:c + 1]).then_inc(a2_done, 1)
                        act.wait_ge(e2a_done, q + 1)
                        act.activation(e2[:, :, 1:T + 1], e2[:, :, 1:T + 1], ACT.Exp).then_inc(e2_done, 1)
                        act.activation(aA[:, :, :], aA[:, :, :], ACT.Exp, scale=-1.0).then_inc(aA_done, 1)
                        act.wait_ge(emin, q + 1)
                        act.activation(dE[:, :, :], dE[:, :, :], ACT.Exp, scale=-1.0).then_inc(dE_done, 1)
                    if rest:
                        act.wait_ge(ht_done, s)
                        hidden_hi(act, G0_)
                    if routed:
                        act.wait_ge(lg_done, 2 * q - 2)
                        act.activation(lg[:, :, :].rearrange("p b e -> p (b e)")[:, bass.ds((2 * q - 4) * E, 2 * E)],
                                       bank[6][:, 0:2 * E], ACT.Copy).then_inc(lg_in, 1)
                    if back:
                        ln_norm(act, call_back(q), 2 * q - 2, 1)
                    if front and mid:
                        ln_norm(act, call_front(q), 2 * q + 2, 0)
                    if back:
                        for j in range(2):
                            act.wait_ge(trX, 2 * q + j - 1)
                            if j == 0 and routed:
                                act.wait_ge(stW, 32 * q - 32)
                            act.activation(stage[:, j, 0, :], bank[4 + j][:, :], ACT.Copy).then_inc(hiW, 1)
                    if front:
                        for j in range(2):
                            act.wait_ge(trK, 2 * q + j + 3)
                            act.activation(cj(kS, j)[:, :, 1:T + 1],
                                           bank[j][:, :].rearrange("p (c t) -> p c t", c=KC),
                                           ACT.Copy).then_inc(kT_in, 1)
                    if tail:
                        for i in range(2):
                            piece_act(act, s + PF, i, 1, bass.ds((s + i) * PIECE, PIECE))
                        act.wait_ge(g_done, s + 1)
                        wait(act, a1_done, s)
                        gate_out(act, G0_)
                        act.wait_ge(ht_done, s + 1)
                        hidden_hi(act, G0_)
                mixed_pairs(act, step)

            @block.gpsimd
            def _(pool):
                def step(q, front, mid, back, routed, tail, rest):
                    if mid:
                        pool.wait_ge(o_scan, q + 1)
                        pool.tensor_tensor(a2[:, :, 1:T + 1], oS[:, :, 0:T], oS[:, :, 1:T + 1],
                                           ALU.subtract).then_inc(d2_done, 1)
                        pool.tensor_tensor(e2[:, :, 1:T + 1], kS[:, :, 1:T + 1], oS[:, :, 1:T + 1],
                                           ALU.subtract).then_inc(e2a_done, 1)
                    if back:
                        ln_pool(pool, call_back(q), 1)
                    if front and mid:
                        ln_pool(pool, call_front(q), 0)
                    if mid:
                        pool.wait_ge(e2_done, q + 1)
                        pool.wait_ge(v_in, 16 * q + 16)
                        pool.tensor_tensor(e2v[:, :, 1:T + 1], e2[:, :, 1:T + 1], vS[:, :, :],
                                           ALU.mult).then_inc(e2v_done, 1)
                        pool.wait_ge(dE_done, q + 1)
                        pool.wait_ge(e2v_done, q + 1)
                        pool.tensor_tensor(vS[:, :, :], dE[:, :, :], vS[:, :, :], ALU.mult).then_inc(ev_done, 1)
                        pool.wait_ge(pscan, q + 1)
                        pool.tensor_tensor(pS[:, :, 0:T], pS[:, :, 0:T], aA[:, :, :], ALU.mult).then_inc(pm_done, 1)
                        pool.wait_ge(ev_done, q + 1)
                        pool.wait_ge(pm_done, q + 1)
                        pool.tensor_tensor(pS[:, :, 0:T], pS[:, :, 0:T], vS[:, :, :], ALU.add).then_inc(num_done, 1)
                    if tail:
                        for i in range(2):
                            piece_pool(pool, 2 * q - 4 + i + PF, i, 1, bass.ds((2 * q - 4 + i) * PIECE, PIECE))
                mixed_pairs(pool, step)

            @block.vector
            def _(dve):
                dve.memset(kS[:, :, 0:1], NEG).then_inc(consW, 1)
                for t in (a2, e2, e2v):
                    dve.memset(t[:, :, 0:1], 0.0).then_inc(consW, 1)
                dve.memset(hid[:, I:IP], 0.0).then_inc(consW, 1)
                dve.wait_ge(consW, 5)

                def step(q, front, mid, back, routed, tail, rest):
                    if mid:
                        dve.wait_ge(kT_in, 2 * q + 2)
                        dve.tensor_tensor_scan(flat(oS), flat(wrst), flat(kS), NEG, ALU.add, ALU.max)\
                            .then_inc(o_scan, 1)
                        dve.wait_ge(o_scan, q + 1)
                        for c in range(KC):
                            at = slice(2 * c, 2 * c + 2)
                            dve.scalar_tensor_tensor(out=dE[:, at, :], in0=kS[:, at, 1:T + 1],
                                                     scalar=ucol[:, c:c + 1], in1=oS[:, at, 0:T], op0=ALU.add,
                                                     op1=ALU.subtract).then_inc(d_done, 1)
                    s = 2 * q - 4
                    if rest:
                        dve.wait_ge(yF_done, s - 1)
                        add_up(dve, s - 2, Y0_)
                    if back:
                        for j in range(2):
                            dve.wait_ge(trY, 2 * q + j - 1)
                            dve.tensor_tensor(xres[:, 2 * q + j - 2, :], xres[:, 2 * q + j - 2, :],
                                              bank[j][:, :], ALU.add).then_inc(res_done, 1)
                        wait_apart(dve, res_done, 2 * q)
                        ln_stats(dve, call_back(q), 2 * q - 2, 1)
                    if rest:
                        dve.wait_ge(tg_done, s)
                        gated(dve, G0_)
                        dve.wait_ge(u_done, s)
                        dve.wait_ge(a1_done, s)
                        hidden(dve, s - 1, U0_)
                    if front and mid:
                        ln_stats(dve, call_front(q), 2 * q + 2, 0)
                    if mid:
                        dve.wait_ge(a2_done, KC * q + KC)
                        dve.wait_ge(e2_done, q + 1)
                        dve.tensor_tensor_scan(flat(qS), flat(a2), flat(e2), 0.0, ALU.mult, ALU.add)\
                            .then_inc(qscan, 1)
                        dve.wait_ge(aA_done, q + 1)
                        dve.wait_ge(qscan, q + 1)
                        dve.tensor_tensor(qS[:, :, 0:T], qS[:, :, 0:T], aA[:, :, :], ALU.mult).then_inc(qm_done, 1)
                        dve.wait_ge(dE_done, q + 1)
                        dve.wait_ge(qm_done, q + 1)
                        dve.tensor_tensor(qS[:, :, 0:T], qS[:, :, 0:T], dE[:, :, :], ALU.add).then_inc(den_done, 1)
                        dve.wait_ge(e2v_done, q + 1)
                        dve.tensor_tensor_scan(flat(pS), flat(a2), flat(e2v), 0.0, ALU.mult, ALU.add)\
                            .then_inc(pscan, 1)
                    if rest:
                        dve.wait_ge(hT_hi, s)
                        hidden_lo(dve, G0_)
                    if mid:
                        dve.wait_ge(den_done, q + 1)
                        dve.reciprocal(qS[:, :, 0:T], qS[:, :, 0:T]).then_inc(rec_done, 1)
                    if rest:
                        dve.wait_ge(yF_done, s)
                        add_up(dve, s - 1, Y0_)
                    if tail:
                        dve.wait_ge(tg_done, s + 1)
                        gated(dve, G0_)
                        dve.wait_ge(u_done, s + 1)
                        dve.wait_ge(a1_done, s + 1)
                        hidden(dve, s, U0_)
                    if tail:
                        dve.wait_ge(hT_hi, s + 1)
                        hidden_lo(dve, G0_)
                    if back:
                        for j in range(2):
                            dve.wait_ge(hiW, 2 * q + j - 1)
                            dve.tensor_tensor(stage[:, j, 1, :], bank[4 + j][:, :], stage[:, j, 0, :].bitcast(F32),
                                              ALU.subtract).then_inc(loW, 1)
                    if mid:
                        dve.wait_ge(rec_done, q + 1)
                        dve.wait_ge(num_done, q + 1)
                        dve.tensor_tensor(vS[:, :, :], pS[:, :, 0:T], qS[:, :, 0:T], ALU.mult).then_inc(y_done, 1)
                mixed_pairs(dve, step)

        (mx_done, lgs_done, ex16, sm_done, rs_done, pr_done, m8_done, gt_done, eq_done, cnt_done, run_done,
         rank_done, left_done, sel_done, selg_done, comb_done) = (
             sem(n) for n in ("mx_done", "lgs_done", "ex16", "sm_done", "rs_done", "pr_done", "m8_done", "gt_done",
                              "eq_done", "cnt_done", "run_done", "rank_done", "left_done", "sel_done", "selg_done",
                              "comb_done"))

        def routing(dve):
            over = lambda t: t.unsqueeze(2).to_broadcast([P, B, E])
            dve.memset(flat(run), 1.0).then_inc(run_done, 1)
            dve.reduce_max(mx[:, :], lg[:, :, :], AX.X).then_inc(mx_done, 1)
            dve.wait_ge(run_done, 1)
            dve.memset(run[:, :, 0:1], 0.0).then_inc(run_done, 1)
            dve.wait_ge(mx_done, 1)
            dve.tensor_tensor(lg[:, :, :], lg[:, :, :], over(mx[:, :]), ALU.subtract).then_inc(lgs_done, 1)
            dve.wait_ge(ex16, 1)
            dve.reduce_sum(sm[:, :], pr[:, :, :], AX.X).then_inc(sm_done, 1)
            dve.wait_ge(sm_done, 1)
            dve.reciprocal(rsm[:, :], sm[:, :]).then_inc(rs_done, 1)
            dve.wait_ge(rs_done, 1)
            dve.tensor_tensor(pr[:, :, :], pr[:, :, :], over(rsm[:, :]), ALU.mult).then_inc(pr_done, 1)
            dve.wait_ge(pr_done, 1)
            for b in range(B):
                dve.max(m8[:, b, :], pr[:, b, :]).then_inc(m8_done, 1)
            sixth = m8[:, :, TOPK - 1]
            dve.wait_ge(m8_done, B)
            dve.tensor_tensor(gt[:, :, :], pr[:, :, :], over(sixth), ALU.is_gt).then_inc(gt_done, 1)
            dve.tensor_tensor(eq[:, :, :], pr[:, :, :], over(sixth), ALU.is_equal).then_inc(eq_done, 1)
            dve.wait_ge(gt_done, 1)
            dve.reduce_sum(cnt[:, :], gt[:, :, :], AX.X).then_inc(cnt_done, 1)
            dve.wait_ge(eq_done, 1)
            dve.wait_ge(run_done, 2)
            dve.tensor_tensor_scan(flat(rank), flat(run), flat(eq), 0.0, ALU.mult, ALU.add).then_inc(rank_done, 1)
            dve.wait_ge(rank_done, 1)
            dve.wait_ge(cnt_done, 1)
            dve.tensor_tensor(rank[:, :, :], rank[:, :, :], over(cnt[:, :]), ALU.add).then_inc(left_done, 1)
            dve.wait_ge(left_done, 1)
            dve.scalar_tensor_tensor(out=eq[:, :, :], in0=rank[:, :, :], scalar=TOPK + 0.5, in1=eq[:, :, :],
                                     op0=ALU.is_lt, op1=ALU.mult).then_inc(sel_done, 1)
            dve.wait_ge(sel_done, 1)
            dve.tensor_tensor(eq[:, :, :], eq[:, :, :], gt[:, :, :], ALU.add).then_inc(selg_done, 1)
            dve.wait_ge(selg_done, 1)
            dve.scalar_tensor_tensor(out=comb[:, NE - E:NE, :].rearrange("p e b -> p b e"), in0=eq[:, :, :], scalar=0.5,
                                     in1=pr[:, :, :], op0=ALU.mult, op1=ALU.mult).then_inc(comb_done, 1)

        GATE, UP, HT_, YF = bank[0:2], bank[2:4], bank[4], bank[5:7]

        def experts(eng, step):
            for b in range(EARLY, B):
                step(b, b % 2, b, 0, 0, True, b > EARLY, True)
            step(B, 0, 0, 1, 0, True, True, True)

            def group(base, gp, last, split, next_split):
                with eng.Fori(1, B - 2, 2) as b:
                    s = eng.snap(base + b)
                    step(s, 1, b, gp, gp, True, True, split)
                    step(s + 1, 0, b + 1, gp, gp, True, True, split)
                step(base + B - 1, 1, B - 1, gp, gp, True, True, split)
                step(base + B, 0, 0, 1 - gp, gp, not last, True, next_split)

            with eng.Fori(B, NSTEP_F - 5 * B + 1, 2 * B) as base:
                group(base, 1, False, True, True)
                group(base + B, 0, False, True, True)
            group(NSTEP_F - 3 * B, 1, False, True, True)
            group(NSTEP_F - 2 * B, 0, False, True, False)
            group(NSTEP_F - B, 1, True, False, False)

        with nc.Block() as block:
            @block.sync
            def _(sp):
                def step(s, par, b, fw, bw, front, back, split):
                    if not front:
                        return
                    if split:
                        sp.wait_ge(piece_lo, PF + s - 1)
                        sp.dma_start(raw[:, par, :], weights[s + PF]).then_inc(piece_in[par], 16)
                    else:
                        sp.wait_ge(u_done, s - 1)
                    if isinstance(s, int) and s == EARLY:
                        sp.wait_ge(stW, 16 * B)
                    else:
                        sp.dma_start(flat_tile(xT[:, par, :, :]), xT_ffn[b]).then_inc(fT_in[par], 16)
                experts(sp, step)

            @block.tensor
            def _(pe):
                def step(s, par, b, fw, bw, front, back, split):
                    if front:
                        if isinstance(b, int) and b == 0:
                            pe.wait_ge(piece_hi, s + PF)
                            pe.wait_ge(piece_lo, s + PF)
                        pe.wait_ge(fT_in[par], 8 * (s - par) + 16)
                        first(pe, par, fw, 0, GATE[par], g_done)
                    if back:
                        pe.wait_ge(hid_done, s)
                        hidden_transposes(pe, HT_)
                    if front:
                        first(pe, par, fw, 1, UP[par], u_done)
                    if back:
                        pe.wait_ge(hT_hi, s)
                        pe.wait_ge(hT_lo, s)
                        second(pe, bw, YF[1 - par])
                experts(pe, step)

            @block.scalar
            def _(act):
                def step(s, par, b, fw, bw, front, back, split):
                    if back:
                        act.wait_ge(ht_done, s)
                        hidden_hi(act, HT_)
                    if front:
                        act.wait_ge(g_done, s + 1)
                        wait(act, a1_done, s)
                        gate_out(act, GATE[par])
                    if front and split:
                        act.wait_ge(u_done, s + 1)
                        piece_act(act, s + PF - par, par, 1 - fw, bass.ds(b * PIECE, PIECE))
                act.wait_ge(lgs_done, 1)
                act.activation(pr[:, :, :], lg[:, :, :], ACT.Exp).then_inc(ex16, 1)
                experts(act, step)

            @block.gpsimd
            def _(pool):
                def step(s, par, b, fw, bw, front, back, split):
                    if front and split:
                        piece_pool(pool, s + PF, par, 1 - fw, bass.ds(b * PIECE, PIECE))
                experts(pool, step)
                with pool.Fori(0, B) as b:
                    pool.wait_ge(added, b + NSTEP_F - B + 1)
                    pool.dma_start(out[b], xres[:, b, :]).then_inc(stored, 16)
                pool.wait_ge(stored, 16 * B)

            @block.vector
            def _(dve):
                routing(dve)

                def step(s, par, b, fw, bw, front, back, split):
                    if back:
                        dve.wait_ge(hT_hi, s)
                        hidden_lo(dve, HT_)
                    if front:
                        dve.wait_ge(tg_done, s + 1)
                        gated(dve, GATE[par])
                        if isinstance(s, int) and s == B:
                            dve.wait_ge(comb_done, 1)
                        dve.wait_ge(u_done, s + 1)
                        dve.wait_ge(a1_done, s + 1)
                        wait(dve, ht_done, s)
                        hidden(dve, s, UP[par])
                    if back:
                        dve.wait_ge(yF_done, s)
                        bb = b - 1 if not isinstance(b, int) else (b - 1) % B
                        add_up(dve, bb, YF[1 - par])
                experts(dve, step)


def kernel(**inputs):
    import numpy as np
    import concourse.bacc as bacc
    from concourse.bass_utils import run_bass_kernel_spmd

    a = {k: np.asarray(v) for k, v in inputs.items()}
    nc = bacc.Bacc("TRN2", target_bir_lowering=False, num_devices=1)

    def chunks(m):
        return m.reshape(-1, P, m.shape[1]).transpose(1, 0, 2).reshape(P, -1)

    groups = []
    for g in range(NG):
        r = slice(g * HG * DH, (g + 1) * HG * DH)
        qk = np.concatenate([a["L0_attn_wq"][r].T, a["L0_attn_wk"][r].T], axis=1)
        used = [chunks(qk), chunks(a["L0_attn_wv"][r].T), chunks(a["L0_attn_wo"][:, r].T)]
        pad = WCOLS - sum(u.shape[1] for u in used)
        groups.append(np.concatenate(used + [np.zeros((P, pad), np.float32)], axis=1))
    ups, downs = [], []
    sw1, sw2 = a["L0_ffn_shared_w1"], a["L0_ffn_shared_w2"]
    for h in range(2):
        ups.append(np.concatenate([sw1[h * I:(h + 1) * I], sw1[(2 + h) * I:(3 + h) * I]], axis=0))
        downs.append(sw2[:, h * I:(h + 1) * I])
    ups += [a["L0_ffn_w1"][e] for e in range(E)]
    downs += [a["L0_ffn_w2"][e] for e in range(E)]
    for up, down in zip(ups, downs):
        w2 = np.concatenate([down.T, np.zeros((IP - I, D), np.float32)], axis=0)
        groups.append(np.concatenate([chunks(up.T), chunks(w2)], axis=1))
    weights = np.stack(groups).reshape(len(groups), P, B, PIECE).transpose(0, 2, 1, 3).reshape(-1, P, PIECE)

    arrays = {
        "x": a["x"],
        "ctxT": a["ctx_2048"].reshape(NQ, 2, T, KC, P).transpose(0, 4, 3, 1, 2).reshape(NQ, P, KC * 2 * T),
        "weights": weights,
        "qw": a["L0_attn_q_norm_w"],
        "kw": a["L0_attn_k_norm_w"],
        "cos": a["L0_attn_rope_cos"][:NH].reshape(-1),
        "sin": a["L0_attn_rope_sin"][:NH].reshape(-1),
        "wkv_w": a["L0_xattn_w"].reshape(KC, P).T,
        "wkv_u": a["L0_xattn_u"].reshape(KC, P).T,
        "gateT": chunks(a["L0_ffn_gate_w"].T),
    }
    feed, args = {}, []
    for name, v in arrays.items():
        v = np.ascontiguousarray(v)
        feed[f"in_{name}"] = v
        args.append(nc.dram_tensor(f"in_{name}", v.shape, mybir.dt.from_np(v.dtype), kind="ExternalInput").ap())
    args.append(nc.dram_tensor("out_x", (B, T, D), F32, kind="ExternalOutput").ap())
    build(nc, *args)
    r = run_bass_kernel_spmd(nc, [feed], core_ids=[0])
    return r.results[0]["out_x"]
```
